# Optimizing a Trainium2 kernel written in Bass

```python
import numpy as np
import jax
import jax.numpy as jnp

def _softmax(x, axis=-1):
    return jax.nn.softmax(x, axis=axis)
def _gelu(x):
    return jax.nn.gelu(x, approximate=True)
def _silu(x):
    return jax.nn.silu(x)
def _sigmoid(x):
    return jax.nn.sigmoid(x)
def _layernorm(x, axis=-1, eps=1e-5):
    m = jnp.mean(x, axis=axis, keepdims=True)
    v = jnp.var(x, axis=axis, keepdims=True)
    return (x - m) / jnp.sqrt(v + eps)
def _scatter_add(tgt, idx, src, axis=0):
    return tgt.at[idx].add(src)
def _segment_sum(src, seg, n):
    return jax.ops.segment_sum(src, seg, n)

kernel_name = 'mk_conv_preact_d1_conv_nhwc192_6e5b9d'

def setup_inputs(seed: int = 0):
    np.random.seed(seed)
    _w = jnp.asarray
    def _rec_inputs():
        import jax
        import jax.numpy as jnp
        _gk = jax.random.key(seed)
        x = -4.65e-05 + 0.9999 * jax.random.normal(jax.random.fold_in(_gk, 1), (4, 256, 256, 192), jnp.float32)
        return x
    x = _rec_inputs()
    def _L0_conv_setup():
        import jax, jax.numpy as jnp
        import numpy as np
        WS = 8
        DR = 2
        HD = 32
        NHEAD = 6
        C = 192
        SHIFT = WS // 2
        DP = WS // DR
        NQ = WS * WS
        NK = DP * DP

        def _rel_index():
            coords = np.array([[i, j] for i in range(WS) for j in range(WS)])
            idx = coords[:, None, :] - coords[None, :, :] + WS - 1
            idx = idx[:, :WS * WS // DR // DR, :]
            return idx

        def _shift_mask(nh, nw):
            p, r, s = (WS, DR, WS - SHIFT)
            m = np.zeros((nh, nw, p, p, p // r, p // r), dtype=bool)
            m[-1, :, :s, :, s // r:, :] = True
            m[-1, :, s:, :, :s // r, :] = True
            m[:, -1, :, :s, :, s // r:] = True
            m[:, -1, :, s:, :, :s // r] = True
            return m.reshape(1, 1, nh * nw, p * p, (p // r) ** 2)
        key = jax.random.key(seed)
        ks = jax.random.split(key, 10)
        d = {}
        d['x'] = jax.random.normal(ks[0], (4, 256, 256, C), dtype=jnp.float32)
        sc = C ** (-0.5)
        d['Wq'] = jax.random.normal(ks[1], (C, C), dtype=jnp.float32) * sc
        d['bq'] = jax.random.normal(ks[2], (C,), dtype=jnp.float32) * 0.01
        d['Wk'] = jax.random.normal(ks[3], (C, C), dtype=jnp.float32) * sc
        d['bk'] = jax.random.normal(ks[4], (C,), dtype=jnp.float32) * 0.01
        d['Wv'] = jax.random.normal(ks[5], (C, C), dtype=jnp.float32) * sc
        d['bv'] = jax.random.normal(ks[6], (C,), dtype=jnp.float32) * 0.01
        d['Wo'] = jax.random.normal(ks[7], (C, C), dtype=jnp.float32) * sc
        d['bo'] = jax.random.normal(ks[8], (C,), dtype=jnp.float32) * 0.01
        d['rel_table'] = jax.random.normal(ks[9], (NHEAD, 2 * WS - 1, 2 * WS - 1), dtype=jnp.float32) * 0.02
        return d
    _L0_conv_all = _L0_conv_setup()
    _L0_conv_in = {k: v for k, v in _L0_conv_all.items() if k in ('Wq', 'bq', 'Wk', 'bk', 'Wv', 'bv', 'Wo', 'bo', 'rel_table', )}
    del _L0_conv_all

    return {
        "x": x,
        "L0_conv_Wq": _L0_conv_in["Wq"],
        "L0_conv_bq": _L0_conv_in["bq"],
        "L0_conv_Wk": _L0_conv_in["Wk"],
        "L0_conv_bk": _L0_conv_in["bk"],
        "L0_conv_Wv": _L0_conv_in["Wv"],
        "L0_conv_bv": _L0_conv_in["bv"],
        "L0_conv_Wo": _L0_conv_in["Wo"],
        "L0_conv_bo": _L0_conv_in["bo"],
        "L0_conv_rel_table": _L0_conv_in["rel_table"],
    }

def reference(x, L0_conv_Wq, L0_conv_bq, L0_conv_Wk, L0_conv_bk, L0_conv_Wv, L0_conv_bv, L0_conv_Wo, L0_conv_bo, L0_conv_rel_table):
    import jax
    import jax.numpy as jnp
    def _L0_conv_ref(x, Wq, bq, Wk, bk, Wv, bv, Wo, bo, rel_table):
        import jax, jax.numpy as jnp
        import numpy as np
        WS = 8
        DR = 2
        HD = 32
        NHEAD = 6
        C = 192
        SHIFT = WS // 2
        DP = WS // DR
        NQ = WS * WS
        NK = DP * DP

        def _rel_index():
            coords = np.array([[i, j] for i in range(WS) for j in range(WS)])
            idx = coords[:, None, :] - coords[None, :, :] + WS - 1
            idx = idx[:, :WS * WS // DR // DR, :]
            return idx

        def _shift_mask(nh, nw):
            p, r, s = (WS, DR, WS - SHIFT)
            m = np.zeros((nh, nw, p, p, p // r, p // r), dtype=bool)
            m[-1, :, :s, :, s // r:, :] = True
            m[-1, :, s:, :, :s // r, :] = True
            m[:, -1, :, :s, :, s // r:] = True
            m[:, -1, :, s:, :, :s // r] = True
            return m.reshape(1, 1, nh * nw, p * p, (p // r) ** 2)
        b, H, W, c = x.shape
        nh, nw = (H // WS, W // WS)
        x = jnp.roll(x, (-SHIFT, -SHIFT), axis=(1, 2))
        xw = x.reshape(b, nh, WS, nw, WS, c).transpose(0, 1, 3, 2, 4, 5)
        xd = xw.reshape(b, nh, nw, DP, DR, DP, DR, c).max(axis=(4, 6))
        xq = xw.reshape(b, nh * nw, NQ, c)
        xd = xd.reshape(b, nh * nw, NK, c)
        q = (xq @ Wq + bq).reshape(b, nh * nw, NQ, NHEAD, HD).transpose(3, 0, 1, 2, 4)
        k = (xd @ Wk + bk).reshape(b, nh * nw, NK, NHEAD, HD).transpose(3, 0, 1, 2, 4)
        v = (xd @ Wv + bv).reshape(b, nh * nw, NK, NHEAD, HD).transpose(3, 0, 1, 2, 4)
        scale = HD ** (-0.5)
        attn = jnp.einsum('hbwpc,hbwqc->hbwpq', q * scale, k)
        idx = _rel_index()
        bias = rel_table[:, idx[:, :, 0], idx[:, :, 1]]
        attn = attn + bias[:, None, None]
        mask = jnp.asarray(_shift_mask(nh, nw))
        attn = jnp.where(mask, -jnp.inf, attn)
        probs = jax.nn.softmax(attn, axis=-1)
        out = jnp.einsum('hbwpq,hbwqc->hbwpc', probs, v)
        out = out.transpose(1, 2, 3, 0, 4).reshape(b, nh * nw, NQ, NHEAD * HD)
        out = out @ Wo + bo
        out = out.reshape(b, nh, nw, WS, WS, c).transpose(0, 1, 3, 2, 4, 5).reshape(b, H, W, c)
        out = jnp.roll(out, (SHIFT, SHIFT), axis=(1, 2))
        return out

    def _gn(v, G=32, eps=1e-5):
        B_, H_, W_, C_ = v.shape
        g = v.reshape(B_, H_, W_, G, C_ // G)
        m = jnp.mean(g, axis=(1, 2, 4), keepdims=True)
        s = jnp.var(g, axis=(1, 2, 4), keepdims=True)
        return ((g - m) / jnp.sqrt(s + eps)).reshape(v.shape)

    def _ln_c(v, eps=1e-6):
        m = jnp.mean(v, axis=-1, keepdims=True)
        s = jnp.var(v, axis=-1, keepdims=True)
        return (v - m) / jnp.sqrt(s + eps)

    def _ln_t(v, eps=1e-5):
        m = jnp.mean(v, axis=-1, keepdims=True)
        s = jnp.var(v, axis=-1, keepdims=True)
        return (v - m) / jnp.sqrt(s + eps)

    def _to_tokens(v):
        B_, H_, W_, C_ = v.shape
        return v.reshape(B_, H_ * W_, C_)
    def _from_tokens(t, like):
        return t.reshape(like.shape)

    x = x + _L0_conv_ref(_gn(x), L0_conv_Wq, L0_conv_bq, L0_conv_Wk, L0_conv_bk, L0_conv_Wv, L0_conv_bv, L0_conv_Wo, L0_conv_bo, L0_conv_rel_table)
    return x


_drawn_inputs = setup_inputs


def setup_inputs(seed=0):
    import zlib

    import numpy as np

    out = dict(_drawn_inputs(seed))
    spreads = {}
    factors = {'L0_conv_bq': 54.664,
     'L0_conv_bk': 64.0,
     'L0_conv_bv': 7.232,
     'L0_conv_bo': 7.412,
     'L0_conv_rel_table': 8.0}
    for name, (base, spread) in spreads.items():
        noise = np.random.default_rng([zlib.crc32(name.encode()), seed]).standard_normal(out[name].shape)
        drawn = base * np.exp(spread * noise) if base else spread * noise
        out[name] = jnp.asarray(drawn.astype(out[name].dtype))
    for name, factor in factors.items():
        out[name] = (out[name] * factor).astype(out[name].dtype)
    return out
```

```python
import numpy as np
import concourse.bass as bass
from concourse import mybir
from contextlib import ExitStack

F32 = mybir.dt.float32
F16 = mybir.dt.float16
ALU = mybir.AluOpType
ACT = mybir.ActivationFunctionType
AX = mybir.AxisListType

B, H, W, C = 4, 256, 256, 192
WS, SHIFT = 8, 4
HEADS, HD = 6, 32
NQ, NK = WS * WS, (WS // 2) ** 2
GROUPS, GC = 32, 6
EPS = 1e-5
ROWS = H // WS
WB = 8
BLOCKS = W // WS // WB
TOK = WB * NQ
CA, CB = 128, C - 128
HA, HB = CA // HD, CB // HD
KEYS = WB * NK
HK = HEADS * NK
PAIRS = WB // 2
ST = H * W // 128 // ROWS
BIG = 16384.0


def attention_kernel(nc, x, wq, bq, wk, bk, wv, bv, wo, bo, flipped_table, out):
    with ExitStack() as ctx:
        def sb(name, shape, dt=F32):
            return ctx.enter_context(nc.sbuf_tensor(name, shape, dt))

        def sem(name):
            return ctx.enter_context(nc.semaphore(name))

        x_in = [sb(f"x_in{j}", [128, 4, C]) for j in range(BLOCKS)]
        x_out = [sb(f"x_out{j}", [128, 4, C]) for j in range(BLOCKS)]
        pool_dx = sb("pool_dx", [128, 2, C])
        pooled = sb("pooled", [128, C])
        xn_a, xn_b = sb("xn_a", [CA, TOK]), sb("xn_b", [CB + 1, TOK])
        xd_a, xd_b = sb("xd_a", [CA, KEYS]), sb("xd_b", [CB + 1, KEYS])
        q_a, q_b = sb("q_a", [CA, TOK]), sb("q_b", [CB, TOK])
        kbd_a, kbd_b = sb("kbd_a", [CA, WB, HA, NK]), sb("kbd_b", [CB, WB, HB, NK])
        vbt_a, vbt_b = sb("vbt_a", [CA, WB, HEADS, NK]), sb("vbt_b", [CB, WB, HEADS, NK])
        vbd = sb("vbd", [HK, WB, C])
        scores = sb("scores", [128, PAIRS, HEADS, NK])
        top = sb("top", [128, PAIRS * HEADS])
        total = sb("total", [128, PAIRS * HEADS])
        inverse = sb("inverse", [128, PAIRS * HEADS])
        probs_t = sb("probs_t", [HK, TOK])
        at_a, at_b = sb("at_a", [CA, TOK]), sb("at_b", [CB + 1, TOK])
        weights = {n: (sb(f"w{n}_a", [CA, C]), sb(f"w{n}_b", [CB + 1, C])) for n in "qkvo"}
        ident = sb("ident", [128, 128])
        head_mask = sb("head_mask", [128, HEADS])
        two_ident = sb("two_ident", [128, 128], F16)
        mask_left = sb("mask_left", [128, 128], F16)
        mask_left_last = sb("mask_left_last", [128, 128], F16)
        bias32 = sb("bias32", [128, HEADS, NK])
        bias16 = sb("bias16", [128, HEADS, NK], F16)
        bias16_low = sb("bias16_low", [128, HEADS, NK], F16)
        row_mask = sb("row_mask", [128, 2, HEADS, NK], F16)
        col_mask = sb("col_mask", [128, HEADS, NK], F16)
        stat_x = [sb(f"stat_x{k}", [128, ST, C]) for k in range(2)]
        stats = sb("stats", [128, GROUPS, ROWS, 6])
        part = sb("part", [128, GROUPS, 2])
        averager = sb("averager", [128, 128])
        half_eps = sb("half_eps", [128, GROUPS])
        power = sb("power", [128, GROUPS])
        spread = sb("spread", [128, GROUPS])
        group_mv = sb("group_mv", [128, 2, GROUPS])
        group_tmp = sb("group_tmp", [128, GROUPS])
        pick = sb("pick", [128, 2, GROUPS])
        picked = sb("picked", [128, 4, GROUPS])
        norm = sb("norm", [128, 4])
        norm_b = sb("norm_b", [128, 2])

        ps = ctx.enter_context(nc.psum_tensor("ps", [128, 8, 512], F32))
        BX, BQ, BK, BS, BV = 0, 2, 4, 5, 6

        s_const = sem("s_const")
        s_setup = sem("s_setup")
        s_setup_p = sem("s_setup_p")
        s_setup_v = sem("s_setup_v")
        s_bias = sem("s_bias")
        s_x = [sem(f"s_x{j}") for j in range(BLOCKS)]
        s_o = [sem(f"s_o{j}") for j in range(BLOCKS)]
        s_stat = [sem(f"s_stat{k}") for k in range(2)]
        v_stat = [sem(f"v_stat{k}") for k in range(2)]
        v_added = [sem(f"v_added{j}") for j in range(BLOCKS)]
        (p_xt, p_kx, p_q, p_kv, p_s, p_vt, p_pt, p_av, p_wo, p_mean, p_var) = [
            sem(n) for n in "p_xt p_kx p_q p_kv p_s p_vt p_pt p_av p_wo p_mean p_var".split()]
        (a_xn, a_xd, a_q, a_vt, a_exp, a_pt, a_av) = [
            sem(n) for n in "a_xn a_xd a_q a_vt a_exp a_pt a_av".split()]
        (v_pool1, v_pool, v_kv, v_vt, v_max, v_sub, v_sum, v_inv, v_probs, v_part, v_dev, v_var, v_norm,
         v_chain) = [sem(n) for n in ("v_pool1 v_pool v_kv v_vt v_max v_sub v_sum v_inv v_probs v_part "
                                      "v_dev v_var v_norm v_chain").split()]
        g_rstd = sem("g_rstd")

        block = ctx.enter_context(nc.Block())

        def dmas(j, last_row):
            return 2 * (1 if j < BLOCKS - 1 else 2) * (4 if last_row else 1)

        def counted(j, b, rows, full=0):
            usual, last = dmas(j, False), dmas(j, True)
            return 16 * usual * (b * ROWS + rows) + 16 * (last - usual) * (b + full)

        def stat_source(b, i):
            return bass.AP(tensor=x.tensor, offset=(b * H * W + i * ST) * C, ap=[[H * W // 128 * C, 128], [1, ST * C]])

        def pieces(dram, tile, b, i, j, last_row):
            found = []
            for dy in range(2):
                for cy, step in [(k, 4) for k in range(4)] if last_row else [(0, 1)]:
                    for cx, ncx in [(0, 32)] if j < BLOCKS - 1 else [(0, 30), (30, 2)]:
                        row = WS * i + SHIFT + 2 * cy + dy - (H if last_row and cy >= 2 else 0)
                        col = WS * WB * j + SHIFT + 2 * cx - (W if cx else 0)
                        far = [[2 * C, ncx], [2 * W * C, 4], [1, 2 * C]] if step == 1 else [[2 * C, ncx], [1, 2 * C]]
                        found.append((bass.AP(tensor=dram.tensor, offset=((b * H + row) * W + col) * C, ap=far),
                                      tile[4 * cx + cy:4 * (cx + ncx) - 3 + (3 if step == 1 else cy):step,
                                           2 * dy:2 * dy + 2, :].rearrange("p a c -> p (a c)")))
            assert len(found) == dmas(j, last_row)
            return found

        @block.sync
        def _(sp):
            for n, w, bb in (("q", wq, bq), ("k", wk, bk), ("v", wv, bv), ("o", wo, bo)):
                wa, wb = weights[n]
                sp.dma_start(wa[:], w[0:CA, :]).then_inc(s_const, 16)
                sp.dma_start(wb[0:CB, :], w[CA:C, :]).then_inc(s_const, 16)
                sp.dma_start(wb[CB:CB + 1, :], bb.rearrange("(a c) -> a c", a=1)).then_inc(s_const, 16)

            def load(b, i, j, last_row):
                found = pieces(x, x_in[j], b, i, j, last_row)
                for far, near in found:
                    sp.dma_start(near, far).then_inc(s_x[j], 16)

            def store(b, i, j, last_row):
                found = pieces(out, x_out[j], b, i, j, last_row)
                for far, near in found:
                    sp.dma_start(far, near).then_inc(s_o[j], 16)

            for k in range(2):
                sp.dma_start(stat_x[k][:].rearrange("p t c -> p (t c)"), stat_source(0, k)).then_inc(s_stat[k], 16)
            with sp.Fori(1, ROWS // 2) as i:
                for k in range(2):
                    sp.wait_ge(v_stat[k], i)
                    sp.dma_start(stat_x[k][:].rearrange("p t c -> p (t c)"),
                                 stat_source(0, 2 * i + k)).then_inc(s_stat[k], 16)
            for j in range(BLOCKS):
                load(0, 0, j, False)
            for half in range(2):
                for m in range(4):
                    for cx in range(4):
                        for n1 in range(2):
                            qi, qj = m // 2, 2 * cx + m % 2
                            p = 64 * half + 16 * m + 4 * cx
                            far = bass.AP(tensor=flipped_table.tensor, offset=15 * (WS - 1 + qi - n1) + WS - 1 - qj,
                                          ap=[[2 * 15, 4], [15 * 15, HEADS], [1, 8]])
                            sp.dma_start(bias32[p:p + 4, :, 8 * n1:8 * n1 + 8], far).then_inc(s_bias, 16)

            def rows(b, with_stats):
                if with_stats:
                    sp.wait_ge(v_stat[0], b * ROWS + ROWS // 2)
                    sp.dma_start(stat_x[0][:].rearrange("p t c -> p (t c)"), stat_source(b + 1, 0)).then_inc(s_stat[0], 16)
                with sp.Fori(0, ROWS - 2) as i:
                    for j in range(BLOCKS):
                        sp.wait_ge(v_added[j], 2 * (b * ROWS + i + 1))
                        store(b, i, j, False)
                        load(b, i + 1, j, False)
                    if with_stats:
                        sp.wait_ge(v_stat[0], b * ROWS + i + 1 + ROWS // 2)
                        sp.dma_start(stat_x[0][:].rearrange("p t c -> p (t c)"),
                                     stat_source(b + 1, i + 1)).then_inc(s_stat[0], 16)
                i = ROWS - 2
                for j in range(BLOCKS):
                    sp.wait_ge(v_added[j], 2 * (b * ROWS + i + 1))
                    store(b, i, j, False)
                    load(b, i + 1, j, True)
                if with_stats:
                    sp.wait_ge(v_stat[0], b * ROWS + i + 1 + ROWS // 2)
                    sp.dma_start(stat_x[0][:].rearrange("p t c -> p (t c)"),
                                 stat_source(b + 1, i + 1)).then_inc(s_stat[0], 16)
                for j in range(BLOCKS):
                    sp.wait_ge(v_added[j], 2 * (b * ROWS + ROWS))
                    store(b, ROWS - 1, j, True)
                    if with_stats:
                        load(b + 1, 0, j, False)

            with sp.Fori(0, B - 1) as b:
                rows(b, True)
            rows(B - 1, False)
            for j in range(BLOCKS):
                sp.wait_ge(s_o[j], counted(j, B, 0))

        @block.gpsimd
        def _(pool):
            steps = [0]

            def done(ins):
                steps[0] += 1
                ins.then_inc(s_setup_p, 1)
                pool.wait_ge(s_setup_p, steps[0])

            def select(view, pattern, base, cm, op, fill):
                done(nc.gpsimd.affine_select(out=view, in_=view, compare_op=op, fill=fill, base=base,
                                             pattern=pattern, channel_multiplier=cm))

            done(nc.gpsimd.memset(ident[:], 0.0))
            select(ident[:], [[-1, 128]], 0, 1, ALU.not_equal, 1.0)
            done(nc.gpsimd.memset(head_mask[:], 1.0))
            select(head_mask[:], [[-HD, HEADS]], 0, 1, ALU.is_ge, 0.0)
            select(head_mask[:], [[HD, HEADS]], HD - 1, -1, ALU.is_ge, 0.0)
            done(nc.gpsimd.memset(pick[:], 1.0))
            select(pick[:], [[CA, 2], [-GC, GROUPS]], 0, 1, ALU.is_ge, 0.0)
            select(pick[:], [[-CA, 2], [GC, GROUPS]], GC - 1, -1, ALU.is_ge, 0.0)
            for t, fill in ((two_ident, 1.0), (mask_left, BIG), (mask_left_last, BIG)):
                done(nc.gpsimd.memset(t[:], 0.0))
                v = t[:].rearrange("p (a q) -> p a q", a=2)
                if t is mask_left_last:
                    v = v[:, 1:2, :]
                for off in (0, 64):
                    select(v, [[0, v.shape[1]], [-1, 64]], -off, 1, ALU.not_equal, fill)
            for t, kv, bit in ((row_mask[:, 1], "y", 1), (col_mask[:], "x", 0)):
                done(nc.gpsimd.memset(t, 0.0))
            done(nc.gpsimd.memset(row_mask[:, 0], 0.0))
            done(nc.gpsimd.memset(averager[:], 1.0 / 128))
            done(nc.gpsimd.memset(power[:], -0.5))
            nc.gpsimd.memset(half_eps[:], EPS).then_inc(s_setup, 1)
            with pool.Fori(0, B) as b:
                pool.wait_ge(v_var, b + 1)
                nc.gpsimd.tensor_tensor(group_mv[:, 1, :], spread[:], power[:], ALU.pow).then_inc(g_rstd, 1)

        @block.vector
        def _(dve):
            steps = [0]

            def done(ins):
                steps[0] += 1
                ins.then_inc(s_setup_v, 1)
                dve.wait_ge(s_setup_v, steps[0])

            done(nc.vector.memset(xn_b[CB:CB + 1, :], 1.0))
            done(nc.vector.memset(xd_b[CB:CB + 1, :], 1.0))
            done(nc.vector.memset(at_b[CB:CB + 1, :], 1.0))
            done(nc.vector.memset(vbt_a[:], 0.0))
            done(nc.vector.memset(vbt_b[:], 0.0))

            def take_in(k, row, groups):
                for g in groups:
                    last = nc.vector.bn_stats(stats[:, g, row, :], stat_x[k][:, :, GC * g:GC * g + GC])
                return last

            with dve.Fori(0, ROWS // 2) as i:
                for k in range(2):
                    dve.wait_ge(s_stat[k], 16 * i + 16)
                    take_in(k, 2 * i + k, range(GROUPS)).then_inc(v_stat[k], 1)

            dve.wait_ge(s_setup, 1)
            dve.wait_ge(s_bias, 16 * 64)
            iv = ident[:].rearrange("p (r x a y c) -> p r x a y c", r=8, x=2, a=2, y=2, c=2)
            for k, view in enumerate((iv[:, :, :, :, 1, :].rearrange("p r x a c -> p (r x a) c"),
                                      iv[:, :, 1].rearrange("p r a y c -> p r (a y c)"))):
                done(nc.vector.tensor_reduce(top[:, k:k + 1], view, AX.XY, ALU.add))
            for c in range(2):
                done(nc.vector.tensor_scalar(top[:, 2 + c:3 + c], top[:, c:c + 1], -BIG, None, ALU.mult))
                done(nc.vector.tensor_scalar(top[:, 4 + c:5 + c], top[:, c:c + 1], BIG, -BIG, ALU.mult, ALU.add))
            rm = row_mask[:, 1].rearrange("p h (x y z) -> p (h x) y z", x=4, y=2)
            cm = col_mask[:].rearrange("p h (x z) -> p h x z", x=2)
            done(nc.vector.tensor_scalar(rm[:, :, 0], rm[:, :, 0], top[:, 2:3], None, ALU.add))
            done(nc.vector.tensor_scalar(rm[:, :, 1], rm[:, :, 1], top[:, 4:5], None, ALU.add))
            done(nc.vector.tensor_scalar(cm[:, :, 0], cm[:, :, 0], top[:, 3:4], None, ALU.add))
            done(nc.vector.tensor_scalar(cm[:, :, 1], cm[:, :, 1], top[:, 5:6], None, ALU.add))
            for h in range(HEADS):
                source = bias32[:, h].rearrange("p (y x) -> p x y", x=4)
                high, low = (t[:, h].rearrange("p (x y) -> p x y", x=4) for t in (bias16, bias16_low))
                done(nc.vector.tensor_copy(high, source))
                done(nc.vector.tensor_tensor(low, source, high, ALU.subtract))
            nc.vector.tensor_copy(bias16[64:128], bias16_low[64:128]).then_inc(s_setup, 1)

            def normalisation(b):
                count = [0]

                def link(ins):
                    count[0] += 1
                    ins.then_inc(v_chain, 1)
                    dve.wait_ge(v_chain, 11 * b + count[0])

                dve.wait_ge(v_stat[1], ROWS // 2)
                dve.wait_ge(v_stat[0], ROWS // 2 + b * ROWS)
                nc.vector.memset(norm_b[:], 0.0)
                for g in range(GROUPS):
                    last = nc.vector.bn_aggr(part[:, g, :], stats[:, g].rearrange("p r s -> p (r s)"))
                last.then_inc(v_part, 1)
                dve.wait_ge(v_part, b + 1)
                dve.wait_ge(p_mean, b + 1)
                link(nc.vector.tensor_scalar(group_mv[:, 0, :], ps[:, BV + 1, 0:GROUPS], -1.0, None, ALU.mult))
                link(nc.vector.tensor_tensor(group_tmp[:], part[:, :, 0], group_mv[:, 0, :], ALU.add))
                link(nc.vector.tensor_tensor(group_tmp[:], group_tmp[:], group_tmp[:], ALU.mult))
                nc.vector.tensor_tensor(group_tmp[:], group_tmp[:], part[:, :, 1], ALU.add).then_inc(v_dev, 1)
                dve.wait_ge(p_var, b + 1)
                nc.vector.tensor_tensor(spread[:], ps[:, BV + 1, GROUPS:2 * GROUPS], half_eps[:], ALU.add).then_inc(v_var, 1)
                dve.wait_ge(g_rstd, b + 1)
                for k, (which, chunk) in enumerate(((1, 0), (1, 1), (0, 0), (0, 1))):
                    link(nc.vector.tensor_tensor(picked[:, k, :], group_mv[:, which, :], pick[:, chunk, :], ALU.mult))
                for k in range(4):
                    link(nc.vector.tensor_reduce(norm[:, k:k + 1], picked[:, k, :], AX.X, ALU.add))
                nc.vector.tensor_tensor(norm_b[:], norm[:, 0:2], norm[:, 2:4], ALU.mult).then_inc(v_norm, 1)


            def pool_keys(n, j, arrived):
                dve.wait_ge(s_x[j], arrived)
                dve.wait_ge(v_pool, n)
                nc.vector.tensor_tensor(pool_dx[:], x_in[j][:, 0:4:2, :], x_in[j][:, 1:4:2, :], ALU.max).then_inc(v_pool1, 1)
                dve.wait_ge(v_pool1, n + 1)
                dve.wait_ge(p_kx, n)
                nc.vector.tensor_tensor(pooled[:], pool_dx[:, 0], pool_dx[:, 1], ALU.max).then_inc(v_pool, 1)

            def keys_values(n):
                dve.wait_ge(p_kv, n + 1)
                dve.wait_ge(p_s, n)
                dve.wait_ge(p_vt, 4 * n)
                for k, (t, rows, heads, h0) in enumerate(((kbd_a, CA, HA, 0), (kbd_b, CB, HB, 0),
                                                          (vbt_a, CA, HA, 0), (vbt_b, CB, HB, HA))):
                    source = ps[0:rows, BK, KEYS * k:KEYS * k + KEYS].rearrange("p (w n) -> p w n", n=NK)
                    last = nc.vector.tensor_tensor(
                        t[:, :, h0:h0 + heads, :],
                        source[:, :, None, :].to_broadcast([rows, WB, heads, NK]),
                        head_mask[0:rows, None, 0:heads, None].to_broadcast([rows, WB, heads, NK]), ALU.mult)
                    if k == 1:
                        last.then_inc(v_kv, 1)
                last.then_inc(v_vt, 1)

            def softmax(n):
                flat = scores[:].rearrange("p g h n -> p (g h) n")
                source = ps[:, BS, 0:PAIRS * HK].rearrange("p (a n) -> p a n", n=NK)
                wide = [128, PAIRS * HEADS, NK]
                dve.wait_ge(p_s, n + 1)
                dve.wait_ge(v_sub, n)
                nc.vector.tensor_reduce(top[:], source, AX.X, ALU.max).then_inc(v_max, 1)
                dve.wait_ge(v_max, n + 1)
                dve.wait_ge(p_pt, n)
                nc.vector.tensor_tensor(flat, source, top[:, :, None].to_broadcast(wide), ALU.subtract).then_inc(v_sub, 1)
                dve.wait_ge(a_exp, n + 1)
                dve.wait_ge(v_inv, n)
                nc.vector.tensor_reduce(total[:], flat, AX.X, ALU.add).then_inc(v_sum, 1)
                dve.wait_ge(v_sum, n + 1)
                dve.wait_ge(v_probs, n)
                nc.vector.reciprocal(inverse[:], total[:]).then_inc(v_inv, 1)
                dve.wait_ge(v_inv, n + 1)
                nc.vector.tensor_tensor(flat, flat, inverse[:, :, None].to_broadcast(wide), ALU.mult).then_inc(v_probs, 1)

            def add_input(n, j, stored):
                dve.wait_ge(p_wo, n + 1)
                dve.wait_ge(s_o[j], stored)
                for k in range(2):
                    nc.vector.tensor_tensor(x_out[j][:, 2 * k:2 * k + 2, :],
                                            ps[:, BQ + k, 0:2 * C].rearrange("p (m c) -> p m c", m=2),
                                            x_in[j][:, 2 * k:2 * k + 2, :], ALU.add).then_inc(v_added[j], 1)

            def row(b, i, with_stats, last_row):
                for j in range(BLOCKS):
                    n = (b * ROWS + i) * BLOCKS + j
                    softmax(n)
                    if not (last_row and j == BLOCKS - 1):
                        keys_values(n + 1)
                    add_input(n, j, counted(j, b, i))
                    if j < BLOCKS - 2:
                        pool_keys(n + 2, j + 2, counted(j + 2, b, i + 1, int(last_row)))
                    elif not last_row:
                        pool_keys(n + 2, j - 2, counted(j - 2, b, i + 2, (i + 2) // ROWS))
                    if with_stats:
                        if j == 0:
                            dve.wait_ge(s_stat[0], 16 * (ROWS // 2 + b * ROWS + i + 1))
                        last = take_in(0, i, range(8 * j, 8 * j + 8))
                        if j == BLOCKS - 1:
                            last.then_inc(v_stat[0], 1)

            def image(b, with_stats):
                normalisation(b)
                for j in range(2):
                    pool_keys(b * ROWS * BLOCKS + j, j, counted(j, b, 1))
                keys_values(b * ROWS * BLOCKS)
                with dve.Fori(0, ROWS - 1) as i:
                    row(b, i, with_stats, False)
                row(b, ROWS - 1, with_stats, True)

            with dve.Fori(0, B - 1) as b:
                image(b, True)
            image(B - 1, False)

        @block.scalar
        def _(act):
            def split(t, order):
                if order == "cells":
                    return t.rearrange("p (w m c) -> p m w c", w=WB, m=4)
                return t.rearrange("p (m w c) -> p w m c", w=WB, m=4)

            def norm_x(n):
                act.wait_ge(p_xt, n + 1)
                act.wait_ge(p_q, n)
                nc.scalar.activation(xn_a[:], ps[:, BX, :], ACT.Identity, bias=norm_b[:, 0:1], scale=norm[:, 0:1])
                nc.scalar.activation(xn_b[0:CB, :], ps[0:CB, BX + 1, :], ACT.Identity,
                                     bias=norm_b[0:CB, 1:2], scale=norm[0:CB, 1:2]).then_inc(a_xn, 1)

            def norm_keys(n):
                act.wait_ge(p_kx, n + 1)
                act.wait_ge(p_kv, n)
                nc.scalar.activation(xd_a[:],
                                     ps[:, BK, 0:KEYS], ACT.Identity,
                                     bias=norm_b[:, 0:1], scale=norm[:, 0:1])
                nc.scalar.activation(xd_b[0:CB, :],
                                     ps[0:CB, BK, KEYS:2 * KEYS],
                                     ACT.Identity, bias=norm_b[0:CB, 1:2], scale=norm[0:CB, 1:2]).then_inc(a_xd, 1)

            def queries(n):
                act.wait_ge(p_q, n + 1)
                act.wait_ge(p_s, n)
                nc.scalar.activation(split(q_a[:], "cells"), ps[:, BQ, :].rearrange("p (m w c) -> p m w c", w=WB, m=4),
                                     ACT.Copy, scale=HD ** -0.5)
                nc.scalar.activation(split(q_b[:], "cells"),
                                     ps[0:CB, BQ + 1, :].rearrange("p (m w c) -> p m w c", w=WB, m=4),
                                     ACT.Copy, scale=HD ** -0.5).then_inc(a_q, 1)

            def values(n):
                act.wait_ge(p_av, n)
                for k in range(4):
                    act.wait_ge(p_vt, 4 * n + k + 1)
                    nc.scalar.activation(vbd[:, 2 * k:2 * k + 2, :].rearrange("p w c -> p (w c)"),
                                         ps[0:HK, BV + k % 2, 0:2 * C], ACT.Copy).then_inc(a_vt, 1)

            def exps(n):
                act.wait_ge(v_sub, n + 1)
                nc.scalar.activation(scores[:].rearrange("p g h n -> p (g h n)"),
                                     scores[:].rearrange("p g h n -> p (g h n)"), ACT.Exp).then_inc(a_exp, 1)

            def probs(n):
                act.wait_ge(p_pt, n + 1)
                act.wait_ge(p_av, n)
                nc.scalar.activation(probs_t[:], ps[0:HK, BV, :], ACT.Copy).then_inc(a_pt, 1)

            def attended(n):
                act.wait_ge(p_av, n + 1)
                act.wait_ge(p_wo, n)
                nc.scalar.activation(split(at_a[:], "windows"), ps[:, BX, :].rearrange("p (w m c) -> p w m c", w=WB, m=4),
                                     ACT.Copy)
                nc.scalar.activation(split(at_b[0:CB, :], "windows"),
                                     ps[0:CB, BX + 1, :].rearrange("p (w m c) -> p w m c", w=WB, m=4),
                                     ACT.Copy).then_inc(a_av, 1)

            def row(b, i, last_row):
                for j in range(BLOCKS):
                    n = (b * ROWS + i) * BLOCKS + j
                    more = not (last_row and j == BLOCKS - 1)
                    exps(n)
                    values(n)
                    if more:
                        norm_keys(n + 1)
                        norm_x(n + 1)
                    probs(n)
                    if more:
                        queries(n + 1)
                    attended(n)

            def image(b):
                n = b * ROWS * BLOCKS
                act.wait_ge(v_norm, b + 1)
                norm_keys(n)
                norm_x(n)
                queries(n)
                with act.Fori(0, ROWS - 1) as i:
                    row(b, i, False)
                row(b, ROWS - 1, True)

            with act.Fori(0, B) as b:
                image(b)

        @block.tensor
        def _(pe):
            def mm(o, left, right, start, stop):
                return nc.tensor.matmul(o, left, right, start=start, stop=stop, skip_group_check=True)

            def transposes(n, j, arrived):
                pe.wait_ge(s_x[j], arrived)
                pe.wait_ge(v_pool, n + 1)
                pe.wait_ge(v_vt, n)
                nc.tensor.transpose(ps[0:CA, BK, 0:KEYS], pooled[:, 0:CA], ident[:])
                nc.tensor.transpose(ps[0:CB, BK, KEYS:2 * KEYS], pooled[:, CA:C], ident[:]).then_inc(p_kx, 1)
                for m in range(4):
                    nc.tensor.transpose(ps[0:CA, BX, 128 * m:128 * m + 128], x_in[j][:, m, 0:CA], ident[:])
                    last = nc.tensor.transpose(ps[0:CB, BX + 1, 128 * m:128 * m + 128], x_in[j][:, m, CA:C], ident[:])
                last.then_inc(p_xt, 1)

            def project(n):
                pe.wait_ge(a_xd, n + 1)
                for k, w in enumerate("kv"):
                    wa, wb = weights[w]
                    for chunk, (lo, hi) in enumerate(((0, CA), (CA, C))):
                        o = ps[0:hi - lo, BK, (2 * k + chunk) * KEYS:(2 * k + chunk + 1) * KEYS]
                        mm(o, wa[:, lo:hi], xd_a[:], True, False)
                        last = mm(o, wb[:, lo:hi], xd_b[:], False, True)
                last.then_inc(p_kv, 1)
                pe.wait_ge(a_xn, n + 1)
                wa, wb = weights["q"]
                for chunk, (lo, hi) in enumerate(((0, CA), (CA, C))):
                    o = ps[0:hi - lo, BQ + chunk, :]
                    mm(o, wa[:, lo:hi], xn_a[:], True, False)
                    last = mm(o, wb[:, lo:hi], xn_b[:], False, True)
                last.then_inc(p_q, 1)

            def score(n, rho, j):
                pe.wait_ge(v_sub, n)
                pe.wait_ge(a_q, n + 1)
                pe.wait_ge(v_kv, n + 1)
                o = ps[:, BS, 0:PAIRS * HK].rearrange("p (g k) -> p g k", g=PAIRS)
                mm(o, two_ident[:], bias16[:].rearrange("p h n -> p (h n)")[:, None, :].to_broadcast([128, PAIRS, HK]),
                   True, False)
                if rho is not None:
                    flat = row_mask[:].rearrange("p v h n -> p (v h n)")
                    for g in range(PAIRS):
                        mm(o[:, g, :], mask_left[:], flat[:, bass.ds(rho * HK, HK)], False, False)
                if j == BLOCKS - 1:
                    mm(o[:, PAIRS - 1, :], mask_left_last[:], col_mask[:].rearrange("p h n -> p (h n)"), False, False)
                for w in range(WB):
                    p = 64 * (w % 2)
                    mm(o[p:p + 64, w // 2, 0:HA * NK], q_a[:, NQ * w:NQ * w + NQ],
                       kbd_a[:, w].rearrange("p h n -> p (h n)"), False, False)
                    last = mm(o[p:p + 64, w // 2, HA * NK:HK], q_b[:, NQ * w:NQ * w + NQ],
                              kbd_b[:, w].rearrange("p h n -> p (h n)"), False, w >= WB - 2)
                last.then_inc(p_s, 1)

            def values(n):
                pe.wait_ge(v_vt, n + 1)
                pe.wait_ge(a_pt, n)
                for k in range(4):
                    pe.wait_ge(a_vt, 4 * n + k - 1) if k else pe.wait_ge(a_vt, 4 * n)
                    for w in (0, 1):
                        nc.tensor.transpose(ps[0:HK, BV + k % 2, C * w:C * w + CA],
                                            vbt_a[:, 2 * k + w].rearrange("p h n -> p (h n)"), ident[:])
                        last = nc.tensor.transpose(ps[0:HK, BV + k % 2, C * w + CA:C * w + C],
                                                   vbt_b[:, 2 * k + w].rearrange("p h n -> p (h n)"), ident[0:CB, 0:CB])
                    last.then_inc(p_vt, 1)

            def probs(n):
                pe.wait_ge(v_probs, n + 1)
                pe.wait_ge(a_vt, 4 * n + 3)
                for g in range(PAIRS):
                    last = nc.tensor.transpose(ps[0:HK, BV, 128 * g:128 * g + 128],
                                               scores[:, g].rearrange("p h n -> p (h n)"), ident[:])
                last.then_inc(p_pt, 1)

            def attend(n):
                pe.wait_ge(a_pt, n + 1)
                pe.wait_ge(a_vt, 4 * n + 4)
                for w in range(WB):
                    mm(ps[0:CA, BX, NQ * w:NQ * w + NQ], vbd[:, w, 0:CA], probs_t[:, NQ * w:NQ * w + NQ], True, True)
                    last = mm(ps[0:CB, BX + 1, NQ * w:NQ * w + NQ], vbd[:, w, CA:C],
                              probs_t[:, NQ * w:NQ * w + NQ], True, True)
                last.then_inc(p_av, 1)

            def project_out(n):
                pe.wait_ge(a_av, n + 1)
                wa, wb = weights["o"]
                for m in range(4):
                    o = ps[:, BQ + m // 2, C * (m % 2):C * (m % 2) + C]
                    mm(o, at_a[:, 128 * m:128 * m + 128], wa[:], True, False)
                    last = mm(o, at_b[:, 128 * m:128 * m + 128], wb[:], False, True)
                last.then_inc(p_wo, 1)

            def row(b, i, last_row):
                for j in range(BLOCKS):
                    n = (b * ROWS + i) * BLOCKS + j
                    more = not (last_row and j == BLOCKS - 1)
                    nj = (j + 1) % BLOCKS
                    arrived = (counted(nj, b, i + 1, int(last_row)) if nj else
                               counted(nj, b, i + 2, (i + 2) // ROWS))
                    values(n)
                    if more:
                        pe.wait_ge(a_av, n)
                        transposes(n + 1, nj, arrived)
                    probs(n)
                    if more:
                        if j:
                            pe.wait_ge(v_added[j - 1], 2 * (b * ROWS + i + 1))
                        else:
                            pe.wait_ge(v_added[BLOCKS - 1], 2 * (b * ROWS + i))
                        project(n + 1)
                    attend(n)
                    if more:
                        if last_row:
                            score(n + 1, 1, nj)
                        elif nj:
                            score(n + 1, None, nj)
                        else:
                            score(n + 1, (i + 2) // ROWS, nj)
                    project_out(n)

            def image(b):
                n = b * ROWS * BLOCKS
                pe.wait_ge(v_part, b + 1)
                pe.wait_ge(a_vt, 4 * n)
                mm(ps[:, BV + 1, 0:GROUPS], averager[:], part[:, :, 0], True, True).then_inc(p_mean, 1)
                pe.wait_ge(v_dev, b + 1)
                mm(ps[:, BV + 1, GROUPS:2 * GROUPS], averager[:], group_tmp[:], True, True).then_inc(p_var, 1)
                pe.wait_ge(a_av, n)
                pe.wait_ge(v_added[BLOCKS - 1], 2 * b * ROWS)
                transposes(n, 0, counted(0, b, 1))
                project(n)
                score(n, None, 0)
                with pe.Fori(0, ROWS - 1) as i:
                    row(b, i, False)
                row(b, ROWS - 1, True)

            pe.wait_ge(s_const, 16 * 12)
            pe.wait_ge(s_setup, 2)
            with pe.Fori(0, B) as b:
                image(b)


_INS = ["x", "Wq", "bq", "Wk", "bk", "Wv", "bv", "Wo", "bo"]


def kernel(**inputs):
    import concourse.bacc as bacc
    from concourse.bass_utils import run_bass_kernel_spmd

    nc = bacc.Bacc("TRN2", target_bir_lowering=False, num_devices=1)
    arrays = {"x": np.ascontiguousarray(inputs["x"])}
    for name in _INS[1:]:
        arrays[name] = np.ascontiguousarray(inputs["L0_conv_" + name])
    arrays["table"] = np.ascontiguousarray(inputs["L0_conv_rel_table"][:, :, ::-1])
    args = [nc.dram_tensor(n, a.shape, mybir.dt.from_np(a.dtype), kind="ExternalInput").ap() for n, a in arrays.items()]
    args.append(nc.dram_tensor("y", arrays["x"].shape, F32, kind="ExternalOutput").ap())
    attention_kernel(nc, *args)
    result = run_bass_kernel_spmd(nc, [arrays], core_ids=[0])
    return result.results[0]["y"]
```

```python
import numpy as np
import concourse.bass as bass
from concourse import mybir
from contextlib import ExitStack

F32 = mybir.dt.float32
F16 = mybir.dt.float16
ALU = mybir.AluOpType
ACT = mybir.ActivationFunctionType
AX = mybir.AxisListType

B, H, W, C = 4, 256, 256, 192
WS, SHIFT = 8, 4
HEADS, HD = 6, 32
NQ, NK = WS * WS, (WS // 2) ** 2
GROUPS, GC = 32, 6
EPS = 1e-5
ROWS = H // WS
WB = 8
BLOCKS = W // WS // WB
TOK = WB * NQ
CA, CB = 128, C - 128
HA, HB = CA // HD, CB // HD
KEYS = WB * NK
HK = HEADS * NK
PAIRS = WB // 2
ST = H * W // 128 // ROWS
UP = 16.0
SCALE = HD ** -0.5
BIG = 32768.0
SELECT_DVE = (3, 7)


def attention_kernel(nc, x, wq, bq, wk, bk, wv, bv, wo, bo, flipped_table, out):
    with ExitStack() as ctx:
        def sb(name, shape, dt=F32):
            return ctx.enter_context(nc.sbuf_tensor(name, shape, dt))

        def sem(name):
            return ctx.enter_context(nc.semaphore(name))

        x_in = [sb(f"x_in{j}", [128, 4, C]) for j in range(BLOCKS)]
        x_out = [sb(f"x_out{j}", [128, 4, C]) for j in range(BLOCKS)]
        pool_dx = sb("pool_dx", [128, 2, C])
        pooled = sb("pooled", [128, C])
        z_a, z_b = sb("z_a", [CA, TOK]), sb("z_b", [CB, TOK])
        zd_a, zd_b = sb("zd_a", [CA, KEYS]), sb("zd_b", [CB, KEYS])
        xh_a, xl_a, xs_b = (sb(n, [128, TOK], F16) for n in ("xh_a", "xl_a", "xs_b"))
        dh_a, dl_a, ds_b = (sb(n, [128, KEYS], F16) for n in ("dh_a", "dl_a", "ds_b"))
        qh_a, ql_a, qs_b = (sb(n, [128, TOK], F16) for n in ("qh_a", "ql_a", "qs_b"))
        ks_a, ks_b = (sb(n, [128, 2, KEYS], F16) for n in ("ks_a", "ks_b"))
        kbd_a = sb("kbd_a", [128, 2, WB, HA, NK], F16)
        kbd_b = sb("kbd_b", [128, 2, WB, HB, NK], F16)
        v16 = sb("v16", [KEYS, 2, C], F16)
        vbd = sb("vbd", [HK, WB, 2, C], F16)
        scores = sb("scores", [128, PAIRS, HEADS, NK])
        top = sb("top", [128, PAIRS * HEADS])
        total = sb("total", [128, PAIRS * HEADS])
        inverse = sb("inverse", [128, PAIRS * HEADS])
        ph, pl = (sb(n, [HK, TOK], F16) for n in ("ph", "pl"))
        ah_a, al_a, as_b = (sb(n, [128, TOK], F16) for n in ("ah_a", "al_a", "as_b"))
        w16 = {n: sb(f"w16_{n}", [128, 4, C + (CB if n == "k" else 0)], F16) for n in "qkvo"}
        w32_a, w32_b = sb("w32_a", [128, C]), sb("w32_b", [128, C])
        qk_bias = sb("qk_bias", [128, 4])
        row_bias32 = sb("row_bias32", [1, 2, C])
        row_bias = sb("row_bias", [128, 2, C], F16)
        ones_vectors = sb("ones_vectors", [128, 2, 128], F16)
        mask_a = sb("mask_a", [128, HA, NK], F16)
        mask_b = sb("mask_b", [128, HB, NK], F16)
        spread_w = sb("spread_w", [128, WB, 2 * 80 + 48], F16)
        ident = sb("ident", [128, 128])
        head_mask = sb("head_mask", [128, HEADS])
        two_ident = sb("two_ident", [128, 128], F16)
        mask_left = sb("mask_left", [128, 128], F16)
        mask_left_last = sb("mask_left_last", [128, 128], F16)
        bias32 = sb("bias32", [128, HEADS, NK])
        bias16 = sb("bias16", [128, HEADS, NK], F16)
        bias16_low = sb("bias16_low", [128, HEADS, NK], F16)
        row_mask = sb("row_mask", [128, 2, HEADS, NK], F16)
        col_mask = sb("col_mask", [128, HEADS, NK], F16)
        stat_x = [sb(f"stat_x{k}", [128, ST, C]) for k in range(2)]
        stats = sb("stats", [128, GROUPS, ROWS, 6])
        part = sb("part", [128, GROUPS, 2])
        averager = sb("averager", [128, 128])
        half_eps = sb("half_eps", [128, GROUPS])
        power = sb("power", [128, GROUPS])
        spread = sb("spread", [128, GROUPS])
        group_mv = sb("group_mv", [128, 2, GROUPS])
        group_tmp = sb("group_tmp", [128, GROUPS])
        pick = sb("pick", [128, 2, GROUPS])
        picked = sb("picked", [128, 4, GROUPS])
        norm = sb("norm", [128, 4])
        norm_b = sb("norm_b", [128, 2])

        ps = ctx.enter_context(nc.psum_tensor("ps", [128, 8, 512], F32))
        BX, BQ, BK, BS, BV = 0, 2, 4, 5, 6

        s_weight, s_vector = sem("s_weight"), sem("s_vector")
        s_split = sem("s_split")
        s_setup = sem("s_setup")
        s_setup_p = sem("s_setup_p")
        s_setup_v = sem("s_setup_v")
        s_bias = sem("s_bias")
        s_x = [sem(f"s_x{j}") for j in range(BLOCKS)]
        s_o = [sem(f"s_o{j}") for j in range(BLOCKS)]
        s_stat = [sem(f"s_stat{k}") for k in range(2)]
        v_stat = [sem(f"v_stat{k}") for k in range(2)]
        v_added = [sem(f"v_added{j}") for j in range(BLOCKS)]
        (p_kx, p_xt, p_kv, p_qa, p_q, p_s, p_sel, p_pt, p_av, p_wo, p_mean, p_var) = [
            sem(n) for n in "p_kx p_xt p_kv p_qa p_q p_s p_sel p_pt p_av p_wo p_mean p_var".split()]
        (a_zd, a_z, a_kv, a_qa, a_qb, a_sel, a_exp, a_pt, a_ava, a_avb) = [
            sem(n) for n in "a_zd a_z a_kv a_qa a_qb a_sel a_exp a_pt a_ava a_avb".split()]
        (v_pool1, v_pool, v_dh, v_xh, v_ks, v_kbd, v_v, v_q, v_sel, v_max, v_sub, v_sum, v_inv, v_probs, v_pt,
         v_av, v_part, v_dev, v_var, v_norm, v_chain) = [
            sem(n) for n in ("v_pool1 v_pool v_dh v_xh v_ks v_kbd v_v v_q v_sel v_max v_sub v_sum v_inv v_probs "
                             "v_pt v_av v_part v_dev v_var v_norm v_chain").split()]
        g_low = sem("g_low")
        g_rstd = sem("g_rstd")

        block = ctx.enter_context(nc.Block())

        def dmas(j, last_row):
            return 2 * (1 if j < BLOCKS - 1 else 2) * (4 if last_row else 1)

        def counted(j, b, rows, full=0):
            usual, last = dmas(j, False), dmas(j, True)
            return 16 * usual * (b * ROWS + rows) + 16 * (last - usual) * (b + full)

        def stat_source(b, i):
            return bass.AP(tensor=x.tensor, offset=(b * H * W + i * ST) * C, ap=[[H * W // 128 * C, 128], [1, ST * C]])

        def pieces(dram, tile, b, i, j, last_row):
            found = []
            for dy in range(2):
                for cy, step in [(k, 4) for k in range(4)] if last_row else [(0, 1)]:
                    for cx, ncx in [(0, 32)] if j < BLOCKS - 1 else [(0, 30), (30, 2)]:
                        row = WS * i + SHIFT + 2 * cy + dy - (H if last_row and cy >= 2 else 0)
                        col = WS * WB * j + SHIFT + 2 * cx - (W if cx else 0)
                        far = [[2 * C, ncx], [2 * W * C, 4], [1, 2 * C]] if step == 1 else [[2 * C, ncx], [1, 2 * C]]
                        found.append((bass.AP(tensor=dram.tensor, offset=((b * H + row) * W + col) * C, ap=far),
                                      tile[4 * cx + cy:4 * (cx + ncx) - 3 + (3 if step == 1 else cy):step,
                                           2 * dy:2 * dy + 2, :].rearrange("p a c -> p (a c)")))
            assert len(found) == dmas(j, last_row)
            return found

        @block.sync
        def _(sp):
            for k, w in enumerate((wq, wk, wv, wo)):
                if k:
                    sp.wait_ge(s_split, k)
                sp.dma_start(w32_a[:], w[0:CA, :]).then_inc(s_weight, 16)
                for half in (0, CB):
                    sp.dma_start(w32_b[half:half + CB, :], w[CA:C, :]).then_inc(s_weight, 16)
            for k, w in enumerate((bq, bk)):
                column = w.rearrange("(c a) -> c a", a=1)
                sp.dma_start(qk_bias[:, 2 * k:2 * k + 1], column[0:CA]).then_inc(s_vector, 16)
                for half in (0, CB):
                    sp.dma_start(qk_bias[half:half + CB, 2 * k + 1:2 * k + 2], column[CA:C]).then_inc(s_vector, 16)
            for k, w in enumerate((bv, bo)):
                sp.dma_start(row_bias32[:, k, :], w.rearrange("(a c) -> a c", a=1)).then_inc(s_vector, 16)

            def load(b, i, j, last_row):
                found = pieces(x, x_in[j], b, i, j, last_row)
                for far, near in found:
                    sp.dma_start(near, far).then_inc(s_x[j], 16)

            def store(b, i, j, last_row):
                found = pieces(out, x_out[j], b, i, j, last_row)
                for far, near in found:
                    sp.dma_start(far, near).then_inc(s_o[j], 16)

            for k in range(2):
                sp.dma_start(stat_x[k][:].rearrange("p t c -> p (t c)"), stat_source(0, k)).then_inc(s_stat[k], 16)
            with sp.Fori(1, ROWS // 2) as i:
                for k in range(2):
                    sp.wait_ge(v_stat[k], i)
                    sp.dma_start(stat_x[k][:].rearrange("p t c -> p (t c)"),
                                 stat_source(0, 2 * i + k)).then_inc(s_stat[k], 16)
            for j in range(BLOCKS):
                load(0, 0, j, False)
            for half in range(2):
                for m in range(4):
                    for cx in range(4):
                        for n1 in range(2):
                            qi, qj = m // 2, 2 * cx + m % 2
                            p = 64 * half + 16 * m + 4 * cx
                            far = bass.AP(tensor=flipped_table.tensor, offset=15 * (WS - 1 + qi - n1) + WS - 1 - qj,
                                          ap=[[2 * 15, 4], [15 * 15, HEADS], [1, 8]])
                            sp.dma_start(bias32[p:p + 4, :, 8 * n1:8 * n1 + 8], far).then_inc(s_bias, 16)

            def rows(b, with_stats):
                if with_stats:
                    sp.wait_ge(v_stat[0], b * ROWS + ROWS // 2)
                    sp.dma_start(stat_x[0][:].rearrange("p t c -> p (t c)"), stat_source(b + 1, 0)).then_inc(s_stat[0], 16)
                with sp.Fori(0, ROWS - 2) as i:
                    for j in range(BLOCKS):
                        sp.wait_ge(v_added[j], 2 * (b * ROWS + i + 1))
                        store(b, i, j, False)
                        load(b, i + 1, j, False)
                    if with_stats:
                        sp.wait_ge(v_stat[0], b * ROWS + i + 1 + ROWS // 2)
                        sp.dma_start(stat_x[0][:].rearrange("p t c -> p (t c)"),
                                     stat_source(b + 1, i + 1)).then_inc(s_stat[0], 16)
                i = ROWS - 2
                for j in range(BLOCKS):
                    sp.wait_ge(v_added[j], 2 * (b * ROWS + i + 1))
                    store(b, i, j, False)
                    load(b, i + 1, j, True)
                if with_stats:
                    sp.wait_ge(v_stat[0], b * ROWS + i + 1 + ROWS // 2)
                    sp.dma_start(stat_x[0][:].rearrange("p t c -> p (t c)"),
                                 stat_source(b + 1, i + 1)).then_inc(s_stat[0], 16)
                for j in range(BLOCKS):
                    sp.wait_ge(v_added[j], 2 * (b * ROWS + ROWS))
                    store(b, ROWS - 1, j, True)
                    if with_stats:
                        load(b + 1, 0, j, False)

            with sp.Fori(0, B - 1) as b:
                rows(b, True)
            rows(B - 1, False)
            for j in range(BLOCKS):
                sp.wait_ge(s_o[j], counted(j, B, 0))

        @block.gpsimd
        def _(pool):
            steps = [0]

            def done(ins):
                steps[0] += 1
                ins.then_inc(s_setup_p, 1)
                pool.wait_ge(s_setup_p, steps[0])

            def select(view, pattern, base, cm, op, fill):
                done(nc.gpsimd.affine_select(out=view, in_=view, compare_op=op, fill=fill, base=base,
                                             pattern=pattern, channel_multiplier=cm))

            done(nc.gpsimd.memset(ident[:], 0.0))
            select(ident[:], [[-1, 128]], 0, 1, ALU.not_equal, 1.0)
            done(nc.gpsimd.memset(head_mask[:], 1.0))
            select(head_mask[:], [[-HD, HEADS]], 0, 1, ALU.is_ge, 0.0)
            select(head_mask[:], [[HD, HEADS]], HD - 1, -1, ALU.is_ge, 0.0)
            done(nc.gpsimd.memset(pick[:], 1.0))
            select(pick[:], [[CA, 2], [-GC, GROUPS]], 0, 1, ALU.is_ge, 0.0)
            select(pick[:], [[-CA, 2], [GC, GROUPS]], GC - 1, -1, ALU.is_ge, 0.0)
            for t, fill in ((two_ident, UP * UP), (mask_left, BIG), (mask_left_last, BIG)):
                done(nc.gpsimd.memset(t[:], 0.0))
                v = t[:].rearrange("p (a q) -> p a q", a=2)
                if t is mask_left_last:
                    v = v[:, 1:2, :]
                for off in (0, 64):
                    select(v, [[0, v.shape[1]], [-1, 64]], -off, 1, ALU.not_equal, fill)
            for t, kv, bit in ((row_mask[:, 1], "y", 1), (col_mask[:], "x", 0)):
                done(nc.gpsimd.memset(t, 0.0))
            done(nc.gpsimd.memset(row_mask[:, 0], 0.0))
            done(nc.gpsimd.memset(spread_w[:], 0.0))
            select(spread_w[:, :, 80:96], [[-NK, WB], [-1, NK]], 0, 1, ALU.not_equal, 1.0)
            done(nc.gpsimd.memset(ones_vectors[:], 0.0))
            for k, one in enumerate((1.0, UP)):
                for r in (0, 32):
                    done(nc.gpsimd.memset(ones_vectors[r:r + 1, k, :], one))
            done(nc.gpsimd.memset(averager[:], 1.0 / 128))
            done(nc.gpsimd.memset(power[:], -0.5))
            nc.gpsimd.memset(half_eps[:], EPS).then_inc(s_setup, 1)
            def low_parts(n):
                pool.wait_ge(v_dh, n + 1)
                pool.wait_ge(g_low, 4 * n)
                nc.gpsimd.tensor_tensor(dl_a[:], zd_a[:], dh_a[:], ALU.subtract).then_inc(g_low, 1)
                pool.wait_ge(g_low, 4 * n + 1)
                nc.gpsimd.tensor_tensor(ds_b[CB:128, :], zd_b[:], ds_b[0:CB, :], ALU.subtract).then_inc(g_low, 1)
                pool.wait_ge(v_xh, n + 1)
                pool.wait_ge(g_low, 4 * n + 2)
                nc.gpsimd.tensor_tensor(xl_a[:], z_a[:], xh_a[:], ALU.subtract).then_inc(g_low, 1)
                pool.wait_ge(g_low, 4 * n + 3)
                nc.gpsimd.tensor_tensor(xs_b[CB:128, :], z_b[:], xs_b[0:CB, :], ALU.subtract).then_inc(g_low, 1)

            with pool.Fori(0, B) as b:
                pool.wait_ge(v_var, b + 1)
                nc.gpsimd.tensor_tensor(group_mv[:, 1, :], spread[:], power[:], ALU.pow).then_inc(g_rstd, 1)
                with pool.Fori(0, ROWS * BLOCKS) as n:
                    low_parts(b * (ROWS * BLOCKS) + n)

        @block.vector
        def _(dve):
            steps = [0]

            def done(ins):
                steps[0] += 1
                ins.then_inc(s_setup_v, 1)
                dve.wait_ge(s_setup_v, steps[0])

            for t in (*w16.values(), row_bias, ks_b):
                done(nc.vector.memset(t[:], 0.0))
            for k, n in enumerate("qkvo"):
                t = w16[n]
                dve.wait_ge(s_weight, 16 * 3 * (k + 1))
                for w in (w32_a, w32_b):
                    done(nc.vector.tensor_scalar(w[:], w[:], UP, None, ALU.mult))
                rest = slice(0, CB) if n != "o" else slice(CB, 128)
                for slot, w, rows in ((0, w32_a, slice(0, 128)), (2, w32_b, slice(0, 128))):
                    done(nc.vector.tensor_copy(t[:, slot, 0:C], w[:]))
                    rows = rows if slot == 0 else rest
                    done(nc.vector.tensor_tensor(t[rows, slot + 1, 0:C], w[rows, :], t[rows, slot, 0:C], ALU.subtract))
                if n == "k":
                    done(nc.vector.tensor_copy(t[:, :, C:C + CB], t[:, :, CA:C]))
                nc.vector.memset(top[:, 0:1], 0.0).then_inc(s_split, 1)
                dve.wait_ge(s_split, k + 1)
            dve.wait_ge(s_vector, 16 * 8)
            done(nc.vector.tensor_scalar(qk_bias[:], qk_bias[:], UP, None, ALU.mult))
            done(nc.vector.tensor_scalar(row_bias32[:], row_bias32[:], UP, None, ALU.mult))
            done(nc.vector.tensor_copy(row_bias[0:1], row_bias32[:]))
            done(nc.vector.tensor_tensor(row_bias[32:33], row_bias32[:], row_bias[0:1], ALU.subtract))

            def take_in(k, row, groups):
                for g in groups:
                    last = nc.vector.bn_stats(stats[:, g, row, :], stat_x[k][:, :, GC * g:GC * g + GC])
                return last

            with dve.Fori(0, ROWS // 2) as i:
                for k in range(2):
                    dve.wait_ge(s_stat[k], 16 * i + 16)
                    take_in(k, 2 * i + k, range(GROUPS)).then_inc(v_stat[k], 1)

            dve.wait_ge(s_setup, 1)
            dve.wait_ge(s_bias, 16 * 64)
            iv = ident[:].rearrange("p (r x a y c) -> p r x a y c", r=8, x=2, a=2, y=2, c=2)
            for k, view in enumerate((iv[:, :, :, :, 1, :].rearrange("p r x a c -> p (r x a) c"),
                                      iv[:, :, 1].rearrange("p r a y c -> p r (a y c)"))):
                done(nc.vector.tensor_reduce(top[:, k:k + 1], view, AX.XY, ALU.add))
            for c in range(2):
                done(nc.vector.tensor_scalar(top[:, 2 + c:3 + c], top[:, c:c + 1], -BIG, None, ALU.mult))
                done(nc.vector.tensor_scalar(top[:, 4 + c:5 + c], top[:, c:c + 1], BIG, -BIG, ALU.mult, ALU.add))
            rm = row_mask[:, 1].rearrange("p h (x y z) -> p (h x) y z", x=4, y=2)
            cm = col_mask[:].rearrange("p h (x z) -> p h x z", x=2)
            done(nc.vector.tensor_scalar(rm[:, :, 0], rm[:, :, 0], top[:, 2:3], None, ALU.add))
            done(nc.vector.tensor_scalar(rm[:, :, 1], rm[:, :, 1], top[:, 4:5], None, ALU.add))
            done(nc.vector.tensor_scalar(cm[:, :, 0], cm[:, :, 0], top[:, 3:4], None, ALU.add))
            done(nc.vector.tensor_scalar(cm[:, :, 1], cm[:, :, 1], top[:, 5:6], None, ALU.add))
            done(nc.vector.tensor_copy(mask_a[:], head_mask[:, 0:HA, None].to_broadcast([128, HA, NK])))
            done(nc.vector.tensor_tensor(mask_b[:], head_mask[:, 0:HB, None].to_broadcast([128, HB, NK]),
                                         head_mask[:, HB:2 * HB, None].to_broadcast([128, HB, NK]), ALU.add))
            done(nc.vector.tensor_scalar(bias32[:], bias32[:], 1.0 / SCALE, None, ALU.mult))
            for h in range(HEADS):
                source = bias32[:, h].rearrange("p (y x) -> p x y", x=4)
                high, low = (t[:, h].rearrange("p (x y) -> p x y", x=4) for t in (bias16, bias16_low))
                done(nc.vector.tensor_copy(high, source))
                done(nc.vector.tensor_tensor(low, source, high, ALU.subtract))
            nc.vector.tensor_copy(bias16[64:128], bias16_low[64:128]).then_inc(s_setup, 1)

            def normalisation(b):
                count = [0]

                def link(ins):
                    count[0] += 1
                    ins.then_inc(v_chain, 1)
                    dve.wait_ge(v_chain, 11 * b + count[0])

                dve.wait_ge(v_stat[1], ROWS // 2)
                dve.wait_ge(v_stat[0], ROWS // 2 + b * ROWS)
                nc.vector.memset(norm_b[:], 0.0)
                for g in range(GROUPS):
                    last = nc.vector.bn_aggr(part[:, g, :], stats[:, g].rearrange("p r s -> p (r s)"))
                last.then_inc(v_part, 1)
                dve.wait_ge(v_part, b + 1)
                dve.wait_ge(p_mean, b + 1)
                link(nc.vector.tensor_scalar(group_mv[:, 0, :], ps[:, BV + 1, 0:GROUPS], -1.0, None, ALU.mult))
                link(nc.vector.tensor_tensor(group_tmp[:], part[:, :, 0], group_mv[:, 0, :], ALU.add))
                link(nc.vector.tensor_tensor(group_tmp[:], group_tmp[:], group_tmp[:], ALU.mult))
                nc.vector.tensor_tensor(group_tmp[:], group_tmp[:], part[:, :, 1], ALU.add).then_inc(v_dev, 1)
                dve.wait_ge(p_var, b + 1)
                nc.vector.tensor_tensor(spread[:], ps[:, BV + 1, GROUPS:2 * GROUPS], half_eps[:], ALU.add).then_inc(v_var, 1)
                dve.wait_ge(g_rstd, b + 1)
                for k, (which, chunk) in enumerate(((1, 0), (1, 1), (0, 0), (0, 1))):
                    link(nc.vector.tensor_tensor(picked[:, k, :], group_mv[:, which, :], pick[:, chunk, :], ALU.mult))
                for k in range(4):
                    link(nc.vector.tensor_reduce(norm[:, k:k + 1], picked[:, k, :], AX.X, ALU.add))
                nc.vector.tensor_tensor(norm_b[:], norm[:, 0:2], norm[:, 2:4], ALU.mult).then_inc(v_norm, 1)


            def pool_keys(n, j, arrived):
                dve.wait_ge(s_x[j], arrived)
                dve.wait_ge(v_pool, n)
                nc.vector.tensor_tensor(pool_dx[:], x_in[j][:, 0:4:2, :], x_in[j][:, 1:4:2, :], ALU.max).then_inc(v_pool1, 1)
                dve.wait_ge(v_pool1, n + 1)
                dve.wait_ge(p_kx, n)
                nc.vector.tensor_tensor(pooled[:], pool_dx[:, 0], pool_dx[:, 1], ALU.max).then_inc(v_pool, 1)

            def high_parts(n):
                dve.wait_ge(a_zd, n + 1)
                dve.wait_ge(p_kv, n)
                nc.vector.tensor_copy(dh_a[:], zd_a[:])
                nc.vector.tensor_copy(ds_b[0:CB, :], zd_b[:]).then_inc(v_dh, 1)
                dve.wait_ge(a_z, n + 1)
                dve.wait_ge(p_q, n)
                nc.vector.tensor_copy(xh_a[:], z_a[:])
                nc.vector.tensor_copy(xs_b[0:CB, :], z_b[:]).then_inc(v_xh, 1)

            def keys_values(n):
                dve.wait_ge(a_kv, n + 1)
                dve.wait_ge(v_kbd, n)
                nc.vector.scalar_tensor_tensor(ks_a[:, 1, :], ps[:, BK, 0:KEYS], qk_bias[:, 2:3], ks_a[:, 0, :],
                                               ALU.add, ALU.subtract)
                nc.vector.scalar_tensor_tensor(ks_b[0:CB, 1, :], ps[0:CB, BK, KEYS:2 * KEYS], qk_bias[0:CB, 3:4],
                                               ks_b[0:CB, 0, :], ALU.add, ALU.subtract).then_inc(v_ks, 1)
                nc.vector.tensor_tensor(v16[:, 1, :], ps[:, BK, 2 * KEYS:2 * KEYS + C], v16[:, 0, :],
                                        ALU.subtract).then_inc(v_v, 1)
                dve.wait_ge(v_ks, n + 1)
                dve.wait_ge(p_s, n)
                for t, source, mask, heads in ((kbd_a, ks_a, mask_a, HA), (kbd_b, ks_b, mask_b, HB)):
                    wide = [128, 2 * WB, heads, NK]
                    last = nc.vector.tensor_tensor(
                        t[:].rearrange("p s w h n -> p (s w) h n"),
                        source[:].rearrange("p s (w n) -> p (s w) n", n=NK)[:, :, None, :].to_broadcast(wide),
                        mask[:, None, :, :].to_broadcast(wide), ALU.mult)
                last.then_inc(v_kbd, 1)

            def queries(n):
                dve.wait_ge(a_qa, n + 1)
                nc.vector.scalar_tensor_tensor(ql_a[:], ps[:, BQ, :], qk_bias[:, 0:1], qh_a[:], ALU.add, ALU.subtract)
                for half in range(2):
                    cols = slice(TOK // 2 * half, TOK // 2 * (half + 1))
                    dve.wait_ge(a_qb, 2 * n + half + 1)
                    last = nc.vector.scalar_tensor_tensor(
                        qs_b[CB:128, cols], ps[CB * half:CB * half + CB, BQ + 1, 0:TOK // 2],
                        qk_bias[CB * half:CB * half + CB, 1:2], qs_b[0:CB, cols], ALU.add, ALU.subtract)
                last.then_inc(v_q, 1)

            def spread_values(n):
                dve.wait_ge(p_av, n)
                for w in SELECT_DVE:
                    dve.wait_ge(p_sel, WB * n + w + 1)
                    nc.vector.tensor_copy(vbd[:, w].rearrange("p s c -> p (s c)"),
                                          ps[0:HK, BV + w % 2, 0:2 * C]).then_inc(v_sel, 1)

            def probs_low(n):
                dve.wait_ge(a_pt, n + 1)
                dve.wait_ge(p_av, n)
                nc.vector.tensor_tensor(pl[:], ps[0:HK, BS, :], ph[:], ALU.subtract).then_inc(v_pt, 1)

            def attended_low(n):
                dve.wait_ge(p_wo, n)
                dve.wait_ge(a_ava, n + 1)
                nc.vector.tensor_tensor(al_a[:], ps[:, BX, :], ah_a[:], ALU.subtract)
                dve.wait_ge(a_avb, n + 1)
                nc.vector.tensor_tensor(as_b[0:CB, :], ps[CB:128, BX + 1, :], as_b[CB:128, :],
                                        ALU.subtract).then_inc(v_av, 1)

            flat = scores[:].rearrange("p g h n -> p (g h) n")
            wide = [128, PAIRS * HEADS, NK]

            def softmax_head(n):
                source = ps[:, BS, 0:PAIRS * HK].rearrange("p (a n) -> p a n", n=NK)
                dve.wait_ge(p_s, n + 1)
                dve.wait_ge(v_sub, n)
                nc.vector.tensor_reduce(top[:], source, AX.X, ALU.max).then_inc(v_max, 1)
                dve.wait_ge(v_max, n + 1)
                dve.wait_ge(p_pt, n)
                nc.vector.tensor_tensor(flat, source, top[:, :, None].to_broadcast(wide), ALU.subtract).then_inc(v_sub, 1)

            def softmax_tail(n):
                dve.wait_ge(a_exp, n + 1)
                dve.wait_ge(v_inv, n)
                nc.vector.tensor_reduce(total[:], flat, AX.X, ALU.add).then_inc(v_sum, 1)
                dve.wait_ge(v_sum, n + 1)
                dve.wait_ge(v_probs, n)
                nc.vector.reciprocal(inverse[:], total[:]).then_inc(v_inv, 1)
                dve.wait_ge(v_inv, n + 1)
                nc.vector.tensor_tensor(flat, flat, inverse[:, :, None].to_broadcast(wide), ALU.mult).then_inc(v_probs, 1)

            def add_input(n, j, stored):
                dve.wait_ge(p_wo, n + 1)
                dve.wait_ge(s_o[j], stored)
                for k in range(2):
                    nc.vector.scalar_tensor_tensor(x_out[j][:, 2 * k:2 * k + 2, :],
                                                   ps[:, BQ + k, 0:2 * C].rearrange("p (m c) -> p m c", m=2),
                                                   1.0 / (UP * UP), x_in[j][:, 2 * k:2 * k + 2, :],
                                                   ALU.mult, ALU.add).then_inc(v_added[j], 1)

            def row(b, i, with_stats, last_row):
                for j in range(BLOCKS):
                    n = (b * ROWS + i) * BLOCKS + j
                    more = not (last_row and j == BLOCKS - 1)
                    softmax_tail(n)
                    if more:
                        high_parts(n + 1)
                    probs_low(n)
                    spread_values(n)
                    if j < BLOCKS - 2:
                        pool_keys(n + 2, j + 2, counted(j + 2, b, i + 1, int(last_row)))
                    elif not last_row:
                        pool_keys(n + 2, j - 2, counted(j - 2, b, i + 2, (i + 2) // ROWS))
                    if more:
                        keys_values(n + 1)
                        queries(n + 1)
                    attended_low(n)
                    if with_stats:
                        if j == 0:
                            dve.wait_ge(s_stat[0], 16 * (ROWS // 2 + b * ROWS + i + 1))
                        last = take_in(0, i, range(8 * j, 8 * j + 8))
                        if j == BLOCKS - 1:
                            last.then_inc(v_stat[0], 1)
                    if more:
                        softmax_head(n + 1)
                    add_input(n, j, counted(j, b, i))

            def image(b, with_stats):
                normalisation(b)
                for j in range(2):
                    pool_keys(b * ROWS * BLOCKS + j, j, counted(j, b, 1))
                n = b * ROWS * BLOCKS
                high_parts(n)
                keys_values(n)
                queries(n)
                softmax_head(n)
                with dve.Fori(0, ROWS - 1) as i:
                    row(b, i, with_stats, False)
                row(b, ROWS - 1, with_stats, True)

            with dve.Fori(0, B - 1) as b:
                image(b, True)
            image(B - 1, False)

        @block.scalar
        def _(act):
            def norm_x(n):
                act.wait_ge(p_xt, n + 1)
                act.wait_ge(v_xh, n)
                act.wait_ge(g_low, 4 * n)
                nc.scalar.activation(z_a[:], ps[:, BX, :], ACT.Identity, bias=norm_b[:, 0:1], scale=norm[:, 0:1])
                nc.scalar.activation(z_b[:], ps[0:CB, BX + 1, :], ACT.Identity,
                                     bias=norm_b[0:CB, 1:2], scale=norm[0:CB, 1:2]).then_inc(a_z, 1)

            def norm_keys(n):
                act.wait_ge(p_kx, n + 1)
                act.wait_ge(v_dh, n)
                act.wait_ge(g_low, 4 * n)
                nc.scalar.activation(zd_a[:], ps[:, BK, 0:KEYS], ACT.Identity, bias=norm_b[:, 0:1], scale=norm[:, 0:1])
                nc.scalar.activation(zd_b[:], ps[0:CB, BK, KEYS:2 * KEYS], ACT.Identity,
                                     bias=norm_b[0:CB, 1:2], scale=norm[0:CB, 1:2]).then_inc(a_zd, 1)

            def keys_values(n):
                act.wait_ge(p_kv, n + 1)
                act.wait_ge(v_kbd, n)
                act.wait_ge(p_sel, WB * n)
                nc.scalar.activation(ks_a[:, 0, :], ps[:, BK, 0:KEYS], ACT.Identity, bias=qk_bias[:, 2:3])
                nc.scalar.activation(ks_b[:, 0, :], ps[:, BK, KEYS:2 * KEYS], ACT.Identity, bias=qk_bias[:, 3:4])
                nc.scalar.activation(v16[:, 0, :], ps[:, BK, 2 * KEYS:2 * KEYS + C], ACT.Copy).then_inc(a_kv, 1)

            def queries(n):
                act.wait_ge(p_qa, n + 1)
                act.wait_ge(p_s, n)
                nc.scalar.activation(qh_a[:], ps[:, BQ, :], ACT.Identity, bias=qk_bias[:, 0:1]).then_inc(a_qa, 1)
                act.wait_ge(p_q, n + 1)
                for half in range(2):
                    nc.scalar.activation(qs_b[0:CB, TOK // 2 * half:TOK // 2 * (half + 1)],
                                         ps[CB * half:CB * half + CB, BQ + 1, 0:TOK // 2],
                                         ACT.Identity, bias=qk_bias[CB * half:CB * half + CB, 1:2]).then_inc(a_qb, 1)

            def values(n):
                act.wait_ge(p_av, n)
                for w in range(WB):
                    if w not in SELECT_DVE:
                        act.wait_ge(p_sel, WB * n + w + 1)
                        nc.scalar.activation(vbd[:, w].rearrange("p s c -> p (s c)"),
                                             ps[0:HK, BV + w % 2, 0:2 * C], ACT.Copy).then_inc(a_sel, 1)

            def exps(n):
                act.wait_ge(v_sub, n + 1)
                nc.scalar.activation(scores[:].rearrange("p g h n -> p (g h n)"),
                                     scores[:].rearrange("p g h n -> p (g h n)"), ACT.Exp,
                                     scale=SCALE / (UP * UP)).then_inc(a_exp, 1)

            def probs(n):
                act.wait_ge(p_pt, n + 1)
                act.wait_ge(p_av, n)
                nc.scalar.activation(ph[:], ps[0:HK, BS, :], ACT.Copy).then_inc(a_pt, 1)

            def attended(n):
                act.wait_ge(p_av, n + 1)
                act.wait_ge(p_wo, n)
                nc.scalar.activation(ah_a[:], ps[:, BX, :], ACT.Copy).then_inc(a_ava, 1)
                nc.scalar.activation(as_b[CB:128, :], ps[CB:128, BX + 1, :], ACT.Copy).then_inc(a_avb, 1)

            def row(b, i, last_row):
                for j in range(BLOCKS):
                    n = (b * ROWS + i) * BLOCKS + j
                    more = not (last_row and j == BLOCKS - 1)
                    if more:
                        norm_keys(n + 1)
                        norm_x(n + 1)
                    probs(n)
                    values(n)
                    if more:
                        keys_values(n + 1)
                        queries(n + 1)
                    attended(n)
                    if more:
                        exps(n + 1)

            def image(b):
                n = b * ROWS * BLOCKS
                act.wait_ge(v_norm, b + 1)
                norm_keys(n)
                norm_x(n)
                keys_values(n)
                queries(n)
                exps(n)
                with act.Fori(0, ROWS - 1) as i:
                    row(b, i, False)
                row(b, ROWS - 1, True)

            with act.Fori(0, B) as b:
                image(b)

        @block.tensor
        def _(pe):
            def mm(o, left, right, start, stop):
                return nc.tensor.matmul(o, left, right, start=start, stop=stop, skip_group_check=True)

            def tokens(t, w):
                return t.rearrange("p (m w c) -> p m w c", w=WB, c=NK)[:, :, w, :]

            def transposes(n, j, arrived):
                pe.wait_ge(s_x[j], arrived)
                pe.wait_ge(v_pool, n + 1)
                pe.wait_ge(v_v, n)
                nc.tensor.transpose(ps[0:CA, BK, 0:KEYS], pooled[:, 0:CA], ident[:])
                nc.tensor.transpose(ps[0:CB, BK, KEYS:2 * KEYS], pooled[:, CA:C], ident[:]).then_inc(p_kx, 1)
                for m in range(4):
                    columns = [ps[0:rows, BX + k, :].rearrange("p (w m c) -> p w m c", w=WB, c=NK)[:, :, m, :]
                               for k, rows in enumerate((CA, CB))]
                    nc.tensor.transpose(columns[0], x_in[j][:, m, 0:CA], ident[:])
                    last = nc.tensor.transpose(columns[1], x_in[j][:, m, CA:C], ident[:])
                last.then_inc(p_xt, 1)

            def products(o, pairs):
                for k, (left, right) in enumerate(pairs):
                    last = mm(o, left, right, k == 0, k == len(pairs) - 1)
                return last

            def project_keys(n):
                pe.wait_ge(v_dh, n + 1)
                pe.wait_ge(g_low, 4 * n + 2)
                operand = [(0, dh_a), (1, dh_a), (0, dl_a), (2, ds_b), (3, ds_b)]
                for lo in (0, CA):
                    products(ps[:, BK, lo:lo + KEYS], [(w16["k"][:, s, lo:lo + 128], t[:]) for s, t in operand])
                products(ps[:, BK, 2 * KEYS:2 * KEYS + C], [(ones_vectors[:, 0, :], row_bias[:, 0, :])] +
                         [(t[:], w16["v"][:, s, :]) for s, t in operand]).then_inc(p_kv, 1)

            def project_queries(n):
                pe.wait_ge(v_xh, n + 1)
                pe.wait_ge(g_low, 4 * n + 4)
                operand = [(0, xh_a), (1, xh_a), (2, xs_b), (3, xs_b), (0, xl_a)]
                products(ps[:, BQ, :], [(w16["q"][:, s, 0:CA], t[:]) for s, t in operand]).then_inc(p_qa, 1)
                for k, (s, t) in enumerate(operand):
                    for half in range(2):
                        last = mm(ps[CB * half:CB * half + CB, BQ + 1, 0:TOK // 2], w16["q"][:, s, CA:C],
                                  t[:, TOK // 2 * half:TOK // 2 * (half + 1)], k == 0, k == len(operand) - 1)
                last.then_inc(p_q, 1)

            def score(n, rho, j):
                pe.wait_ge(v_sub, n)
                pe.wait_ge(v_pt, n)
                pe.wait_ge(v_q, n + 1)
                pe.wait_ge(v_kbd, n + 1)
                o = ps[:, BS, 0:PAIRS * HK].rearrange("p (g k) -> p g k", g=PAIRS)
                mm(o, two_ident[:], bias16[:].rearrange("p h n -> p (h n)")[:, None, :].to_broadcast([128, PAIRS, HK]),
                   True, False)
                if rho is not None:
                    flat = row_mask[:].rearrange("p v h n -> p (v h n)")
                    for g in range(PAIRS):
                        mm(o[:, g, :], mask_left[:], flat[:, bass.ds(rho * HK, HK)], False, False)
                if j == BLOCKS - 1:
                    mm(o[:, PAIRS - 1, :], mask_left_last[:], col_mask[:].rearrange("p h n -> p (h n)"), False, False)
                for w in range(WB):
                    p = 64 * (w % 2)
                    cols = slice(NQ * w, NQ * w + NQ)
                    k_high, k_low = (kbd_a[:, s, w].rearrange("p h n -> p (h n)") for s in range(2))
                    for left, right in ((qh_a, k_high), (qh_a, k_low), (ql_a, k_high)):
                        mm(o[p:p + 64, w // 2, 0:HA * NK], left[:, cols], right, False, False)
                    for s in range(2):
                        last = mm(o[p:p + 64, w // 2, HA * NK:HK], qs_b[:, cols],
                                  kbd_b[:, s, w].rearrange("p h n -> p (h n)"), False, s == 1 and w >= WB - 2)
                last.then_inc(p_s, 1)

            def selected(n, w):
                if w in SELECT_DVE:
                    pe.wait_ge(v_sel, len(SELECT_DVE) * n + SELECT_DVE.index(w) + 1)
                else:
                    mine = [k for k in range(WB) if k not in SELECT_DVE]
                    pe.wait_ge(a_sel, len(mine) * n + mine.index(w) + 1)

            def values(n):
                pe.wait_ge(v_v, n + 1)
                for w in range(WB):
                    if w < 2:
                        pe.wait_ge(a_sel, (WB - len(SELECT_DVE)) * n)
                        pe.wait_ge(v_sel, len(SELECT_DVE) * n)
                    else:
                        selected(n, w - 2)
                    o = ps[:, BV + w % 2, 0:2 * C].rearrange("p (s c) -> p s c", s=2)
                    for h in range(HEADS):
                        at = 80 - NK * h
                        last = mm(o[:, :, HD * h:HD * h + HD], spread_w[:, w, at:at + 128],
                                  v16[:, :, HD * h:HD * h + HD], True, True)
                    last.then_inc(p_sel, 1)

            def probs(n):
                pe.wait_ge(v_probs, n + 1)
                for g in range(PAIRS):
                    last = nc.tensor.transpose(ps[0:HK, BS, 128 * g:128 * g + 128],
                                               scores[:, g].rearrange("p h n -> p (h n)"), ident[:])
                last.then_inc(p_pt, 1)

            def attend(n):
                pe.wait_ge(v_pt, n + 1)
                selected(n, WB - 2)
                selected(n, WB - 1)
                for w in range(WB):
                    cols = slice(NQ * w, NQ * w + NQ)
                    for bank, c in ((BX, 0), (BX + 1, C - 128)):
                        last = products(tokens(ps[:, bank, :], w), [(vbd[:, w, s, c:c + 128], t[:, cols])
                                                            for s, t in ((0, ph), (0, pl), (1, ph))])
                last.then_inc(p_av, 1)

            def project_out(n):
                pe.wait_ge(v_av, n + 1)
                for m in range(4):
                    cols = slice(128 * m, 128 * m + 128)
                    last = products(ps[:, BQ + m // 2, C * (m % 2):C * (m % 2) + C],
                                    [(ones_vectors[:, 1, :], row_bias[:, 1, :])] +
                                    [(t[:, cols], w16["o"][:, s, :])
                                     for s, t in ((0, ah_a), (1, ah_a), (0, al_a), (2, as_b), (3, as_b))])
                last.then_inc(p_wo, 1)

            def row(b, i, last_row):
                for j in range(BLOCKS):
                    n = (b * ROWS + i) * BLOCKS + j
                    more = not (last_row and j == BLOCKS - 1)
                    nj = (j + 1) % BLOCKS
                    arrived = (counted(nj, b, i + 1, int(last_row)) if nj else
                               counted(nj, b, i + 2, (i + 2) // ROWS))
                    if more:
                        pe.wait_ge(v_av, n)
                        transposes(n + 1, nj, arrived)
                    probs(n)
                    values(n)
                    if more:
                        project_keys(n + 1)
                        if j:
                            pe.wait_ge(v_added[j - 1], 2 * (b * ROWS + i + 1))
                        else:
                            pe.wait_ge(v_added[BLOCKS - 1], 2 * (b * ROWS + i))
                        project_queries(n + 1)
                        pe.wait_ge(a_z, n + 2)
                    attend(n)
                    if more:
                        if last_row:
                            score(n + 1, 1, nj)
                        elif nj:
                            score(n + 1, None, nj)
                        else:
                            score(n + 1, (i + 2) // ROWS, nj)
                    project_out(n)

            def image(b):
                n = b * ROWS * BLOCKS
                pe.wait_ge(v_part, b + 1)
                pe.wait_ge(v_sel, len(SELECT_DVE) * n)
                mm(ps[:, BV + 1, 0:GROUPS], averager[:], part[:, :, 0], True, True).then_inc(p_mean, 1)
                pe.wait_ge(v_dev, b + 1)
                mm(ps[:, BV + 1, GROUPS:2 * GROUPS], averager[:], group_tmp[:], True, True).then_inc(p_var, 1)
                pe.wait_ge(v_av, n)
                pe.wait_ge(v_added[BLOCKS - 1], 2 * b * ROWS)
                transposes(n, 0, counted(0, b, 1))
                project_keys(n)
                project_queries(n)
                score(n, None, 0)
                with pe.Fori(0, ROWS - 1) as i:
                    row(b, i, False)
                row(b, ROWS - 1, True)

            pe.wait_ge(s_setup, 2)
            with pe.Fori(0, B) as b:
                image(b)


_INS = ["x", "Wq", "bq", "Wk", "bk", "Wv", "bv", "Wo", "bo"]


def kernel(**inputs):
    import concourse.bacc as bacc
    from concourse.bass_utils import run_bass_kernel_spmd

    nc = bacc.Bacc("TRN2", target_bir_lowering=False, num_devices=1)
    arrays = {"x": np.ascontiguousarray(inputs["x"])}
    for name in _INS[1:]:
        arrays[name] = np.ascontiguousarray(inputs["L0_conv_" + name])
    arrays["table"] = np.ascontiguousarray(inputs["L0_conv_rel_table"][:, :, ::-1])
    args = [nc.dram_tensor(n, a.shape, mybir.dt.from_np(a.dtype), kind="ExternalInput").ap() for n, a in arrays.items()]
    args.append(nc.dram_tensor("y", arrays["x"].shape, F32, kind="ExternalOutput").ap())
    attention_kernel(nc, *args)
    result = run_bass_kernel_spmd(nc, [arrays], core_ids=[0])
    return result.results[0]["y"]
```

```python
import numpy as np
import concourse.bass as bass
from concourse import mybir
from contextlib import ExitStack

F32 = mybir.dt.float32
F16 = mybir.dt.float16
ALU = mybir.AluOpType
ACT = mybir.ActivationFunctionType
AX = mybir.AxisListType

B, H, W, C = 4, 256, 256, 192
WS, SHIFT = 8, 4
HEADS, HD = 6, 32
NQ, NK = WS * WS, (WS // 2) ** 2
GROUPS, GC = 32, 6
EPS = 1e-5
ROWS = H // WS
WB = 8
BLOCKS = W // WS // WB
TOK = WB * NQ
CA, CB = 128, C - 128
HA, HB = CA // HD, CB // HD
KEYS = WB * NK
HK = HEADS * NK
PAIRS = WB // 2
ST = H * W // 128 // ROWS
UP = 16.0
SCALE = HD ** -0.5
BIG = 32768.0


def attention_kernel(nc, x, wq, bq, wk, bk, wv, bv, wo, bo, flipped_table, out):
    with ExitStack() as ctx:
        def sb(name, shape, dt=F32):
            return ctx.enter_context(nc.sbuf_tensor(name, shape, dt))

        def sem(name):
            return ctx.enter_context(nc.semaphore(name))

        x_in = [sb(f"x_in{j}", [128, 4, C]) for j in range(BLOCKS)]
        x_out = [sb(f"x_out{j}", [128, 4, C]) for j in range(BLOCKS)]
        pool_dx = sb("pool_dx", [128, 2, C])
        pooled = sb("pooled", [128, C])
        z_a, z_b = sb("z_a", [CA, TOK]), sb("z_b", [CB, TOK])
        zd_a, zd_b = sb("zd_a", [CA, KEYS]), sb("zd_b", [CB, KEYS])
        xh_a, xl_a, xs_b = (sb(n, [128, 2, TOK], F16) for n in ("xh_a", "xl_a", "xs_b"))
        dh_a, dl_a, ds_b = (sb(n, [128, KEYS], F16) for n in ("dh_a", "dl_a", "ds_b"))
        qh_a, ql_a, qs_b = (sb(n, [128, TOK], F16) for n in ("qh_a", "ql_a", "qs_b"))
        ks_a, ks_b = (sb(n, [128, 2, KEYS], F16) for n in ("ks_a", "ks_b"))
        kbd_a = sb("kbd_a", [128, 2, WB, HA, NK], F16)
        kbd_b = sb("kbd_b", [128, 2, WB, HB, NK], F16)
        v16 = sb("v16", [KEYS, 2, C], F16)
        vbd = sb("vbd", [HK, 2, WB, 2, C], F16)
        scores = sb("scores", [128, PAIRS, HEADS, NK])
        top = sb("top", [128, PAIRS * HEADS])
        total = sb("total", [128, PAIRS * HEADS])
        inverse = sb("inverse", [128, PAIRS * HEADS])
        ph, pl = (sb(n, [HK, TOK], F16) for n in ("ph", "pl"))
        ah_a, al_a, as_b = (sb(n, [128, TOK], F16) for n in ("ah_a", "al_a", "as_b"))
        w16 = {n: sb(f"w16_{n}", [128, 4, C + (CB if n == "k" else 0)], F16) for n in "qkvo"}
        w32_a, w32_b = sb("w32_a", [128, C]), sb("w32_b", [128, C])
        qk_bias = sb("qk_bias", [128, 4])
        v_bias32 = sb("v_bias32", [1, C])
        v_bias = sb("v_bias", [128, C], F16)
        ones_rows = sb("ones_rows", [128, 128], F16)
        out_bias = sb("out_bias", [128, C])
        mask_a = sb("mask_a", [128, HA, NK], F16)
        mask_b = sb("mask_b", [128, HB, NK], F16)
        spread_w = sb("spread_w", [128, WB, 2 * 80 + 48], F16)
        ident = sb("ident", [128, 128])
        head_mask = sb("head_mask", [128, HEADS])
        two_ident = sb("two_ident", [128, 128], F16)
        mask_left = sb("mask_left", [128, 128], F16)
        mask_left_last = sb("mask_left_last", [128, 128], F16)
        bias32 = sb("bias32", [128, HEADS, NK])
        bias16 = sb("bias16", [128, HEADS, NK], F16)
        bias16_low = sb("bias16_low", [128, HEADS, NK], F16)
        row_mask = sb("row_mask", [128, 2, HEADS, NK], F16)
        col_mask = sb("col_mask", [128, HEADS, NK], F16)
        stat_x = [sb(f"stat_x{k}", [128, ST, C]) for k in range(2)]
        stats = sb("stats", [128, GROUPS, ROWS, 6])
        part = sb("part", [128, GROUPS, 2])
        averager = sb("averager", [128, 128])
        half_eps = sb("half_eps", [128, GROUPS])
        power = sb("power", [128, GROUPS])
        spread = sb("spread", [128, GROUPS])
        group_mv = sb("group_mv", [128, 2, GROUPS])
        group_tmp = sb("group_tmp", [128, GROUPS])
        pick = sb("pick", [128, 2, GROUPS])
        picked = sb("picked", [128, 4, GROUPS])
        norm = sb("norm", [128, 4])
        norm_b = sb("norm_b", [128, 2])

        ps = ctx.enter_context(nc.psum_tensor("ps", [128, 8, 512], F32))
        BX, BQ, BK, BS, BV = 0, 2, 4, 5, 6

        s_weight, s_vector = sem("s_weight"), sem("s_vector")
        s_out_bias, s_bias = sem("s_out_bias"), sem("s_bias")
        s_split = sem("s_split")
        s_setup = sem("s_setup")
        s_setup_p = sem("s_setup_p")
        s_setup_v = sem("s_setup_v")
        s_x = [sem(f"s_x{j}") for j in range(BLOCKS)]
        s_o = [sem(f"s_o{j}") for j in range(BLOCKS)]
        s_stat = [sem(f"s_stat{k}") for k in range(2)]
        v_stat = [sem(f"v_stat{k}") for k in range(2)]
        v_added = [sem(f"v_added{j}") for j in range(BLOCKS)]
        (p_kx, p_xt, p_kv, p_qa, p_q, p_s, p_sel, p_pt, p_av, p_wo, p_mean, p_var) = [
            sem(n) for n in "p_kx p_xt p_kv p_qa p_q p_s p_sel p_pt p_av p_wo p_mean p_var".split()]
        (a_zd, a_z, a_kv, a_qa, a_qb, a_sel, a_exp, a_pt, a_ava, a_avb) = [
            sem(n) for n in "a_zd a_z a_kv a_qa a_qb a_sel a_exp a_pt a_ava a_avb".split()]
        (v_pool1, v_pool, v_dh, v_xh, v_ks, v_v, v_q, v_max, v_sub, v_sum, v_inv, v_pt,
         v_av, v_part, v_dev, v_var, v_norm, v_chain) = [
            sem(n) for n in ("v_pool1 v_pool v_dh v_xh v_ks v_v v_q v_max v_sub v_sum v_inv "
                             "v_pt v_av v_part v_dev v_var v_norm v_chain").split()]
        g_dl, g_xl, g_kbd = sem("g_dl"), sem("g_xl"), sem("g_kbd")
        g_probs, g_bias, g_rstd = sem("g_probs"), sem("g_bias"), sem("g_rstd")

        block = ctx.enter_context(nc.Block())

        def dmas(j, last_row):
            return 2 * (1 if j < BLOCKS - 1 else 2) * (4 if last_row else 1)

        def counted(j, b, rows, full=0):
            usual, last = dmas(j, False), dmas(j, True)
            return 16 * usual * (b * ROWS + rows) + 16 * (last - usual) * (b + full)

        def stat_source(b, i):
            return bass.AP(tensor=x.tensor, offset=(b * H * W + i * ST) * C, ap=[[H * W // 128 * C, 128], [1, ST * C]])

        def pieces(dram, tile, b, i, j, last_row):
            found = []
            for dy in range(2):
                for cy, step in [(k, 4) for k in range(4)] if last_row else [(0, 1)]:
                    for cx, ncx in [(0, 32)] if j < BLOCKS - 1 else [(0, 30), (30, 2)]:
                        row = WS * i + SHIFT + 2 * cy + dy - (H if last_row and cy >= 2 else 0)
                        col = WS * WB * j + SHIFT + 2 * cx - (W if cx else 0)
                        far = [[2 * C, ncx], [2 * W * C, 4], [1, 2 * C]] if step == 1 else [[2 * C, ncx], [1, 2 * C]]
                        found.append((bass.AP(tensor=dram.tensor, offset=((b * H + row) * W + col) * C, ap=far),
                                      tile[4 * cx + cy:4 * (cx + ncx) - 3 + (3 if step == 1 else cy):step,
                                           2 * dy:2 * dy + 2, :].rearrange("p a c -> p (a c)")))
            assert len(found) == dmas(j, last_row)
            return found

        @block.sync
        def _(sp):
            for k, w in enumerate((wq, wk, wv, wo)):
                if k:
                    sp.wait_ge(s_split, k)
                sp.dma_start(w32_a[:], w[0:CA, :]).then_inc(s_weight, 16)
                for half in (0, CB):
                    sp.dma_start(w32_b[half:half + CB, :], w[CA:C, :]).then_inc(s_weight, 16)
            for k, w in enumerate((bq, bk)):
                column = w.rearrange("(c a) -> c a", a=1)
                sp.dma_start(qk_bias[:, 2 * k:2 * k + 1], column[0:CA]).then_inc(s_vector, 16)
                for half in (0, CB):
                    sp.dma_start(qk_bias[half:half + CB, 2 * k + 1:2 * k + 2], column[CA:C]).then_inc(s_vector, 16)
            sp.dma_start(v_bias32[:], bv.rearrange("(a c) -> a c", a=1)).then_inc(s_vector, 16)
            sp.dma_start(out_bias[:], bass.AP(tensor=bo.tensor, offset=0, ap=[[0, 128], [1, C]])).then_inc(s_out_bias, 16)

            def load(b, i, j, last_row):
                found = pieces(x, x_in[j], b, i, j, last_row)
                for far, near in found:
                    sp.dma_start(near, far).then_inc(s_x[j], 16)

            def store(b, i, j, last_row):
                found = pieces(out, x_out[j], b, i, j, last_row)
                for far, near in found:
                    sp.dma_start(far, near).then_inc(s_o[j], 16)

            for k in range(2):
                sp.dma_start(stat_x[k][:].rearrange("p t c -> p (t c)"), stat_source(0, k)).then_inc(s_stat[k], 16)
            with sp.Fori(1, ROWS // 2) as i:
                for k in range(2):
                    sp.wait_ge(v_stat[k], i)
                    sp.dma_start(stat_x[k][:].rearrange("p t c -> p (t c)"),
                                 stat_source(0, 2 * i + k)).then_inc(s_stat[k], 16)
            for j in range(BLOCKS):
                load(0, 0, j, False)
            for half in range(2):
                for m in range(4):
                    for cx in range(4):
                        for n1 in range(2):
                            qi, qj = m // 2, 2 * cx + m % 2
                            p = 64 * half + 16 * m + 4 * cx
                            far = bass.AP(tensor=flipped_table.tensor, offset=15 * (WS - 1 + qi - n1) + WS - 1 - qj,
                                          ap=[[2 * 15, 4], [15 * 15, HEADS], [1, 8]])
                            sp.dma_start(bias32[p:p + 4, :, 8 * n1:8 * n1 + 8], far).then_inc(s_bias, 16)

            def rows(b, with_stats):
                if with_stats:
                    sp.wait_ge(v_stat[0], b * ROWS + ROWS // 2)
                    sp.dma_start(stat_x[0][:].rearrange("p t c -> p (t c)"), stat_source(b + 1, 0)).then_inc(s_stat[0], 16)

                def next_statistics(i):
                    if with_stats:
                        sp.wait_ge(v_stat[0], b * ROWS + i + 1 + ROWS // 2)
                        sp.dma_start(stat_x[0][:].rearrange("p t c -> p (t c)"),
                                     stat_source(b + 1, i + 1)).then_inc(s_stat[0], 16)

                with sp.Fori(0, ROWS - 2) as i:
                    for j in range(BLOCKS):
                        if j == BLOCKS - 1:
                            next_statistics(i)
                        sp.wait_ge(v_added[j], 2 * (b * ROWS + i + 1))
                        load(b, i + 1, j, False)
                        store(b, i, j, False)
                i = ROWS - 2
                for j in range(BLOCKS):
                    if j == BLOCKS - 1:
                        next_statistics(i)
                    sp.wait_ge(v_added[j], 2 * (b * ROWS + i + 1))
                    load(b, i + 1, j, True)
                    store(b, i, j, False)
                for j in range(BLOCKS):
                    sp.wait_ge(v_added[j], 2 * (b * ROWS + ROWS))
                    if with_stats:
                        load(b + 1, 0, j, False)
                    store(b, ROWS - 1, j, True)

            with sp.Fori(0, B - 1) as b:
                rows(b, True)
            rows(B - 1, False)
            for j in range(BLOCKS):
                sp.wait_ge(s_o[j], counted(j, B, 0))

        @block.gpsimd
        def _(pool):
            steps = [0]

            def done(ins):
                steps[0] += 1
                ins.then_inc(s_setup_p, 1)
                pool.wait_ge(s_setup_p, steps[0])

            def select(view, pattern, base, cm, op, fill):
                done(nc.gpsimd.affine_select(out=view, in_=view, compare_op=op, fill=fill, base=base,
                                             pattern=pattern, channel_multiplier=cm))

            done(nc.gpsimd.memset(ident[:], 0.0))
            select(ident[:], [[-1, 128]], 0, 1, ALU.not_equal, 1.0)
            done(nc.gpsimd.memset(head_mask[:], 1.0))
            select(head_mask[:], [[-HD, HEADS]], 0, 1, ALU.is_ge, 0.0)
            select(head_mask[:], [[HD, HEADS]], HD - 1, -1, ALU.is_ge, 0.0)
            done(nc.gpsimd.memset(pick[:], 1.0))
            select(pick[:], [[CA, 2], [-GC, GROUPS]], 0, 1, ALU.is_ge, 0.0)
            select(pick[:], [[-CA, 2], [GC, GROUPS]], GC - 1, -1, ALU.is_ge, 0.0)
            for t, fill in ((two_ident, UP * UP), (mask_left, BIG), (mask_left_last, BIG)):
                done(nc.gpsimd.memset(t[:], 0.0))
                v = t[:].rearrange("p (a q) -> p a q", a=2)
                if t is mask_left_last:
                    v = v[:, 1:2, :]
                for off in (0, 64):
                    select(v, [[0, v.shape[1]], [-1, 64]], -off, 1, ALU.not_equal, fill)
            for t in (row_mask[:, 1], col_mask[:]):
                done(nc.gpsimd.memset(t, 0.0))
            done(nc.gpsimd.memset(row_mask[:, 0], 0.0))
            done(nc.gpsimd.memset(spread_w[:], 0.0))
            select(spread_w[:, :, 80:96], [[-NK, WB], [-1, NK]], 0, 1, ALU.not_equal, 1.0)
            done(nc.gpsimd.memset(ones_rows[:], 0.0))
            for r in (0, 32):
                done(nc.gpsimd.memset(ones_rows[r:r + 1, :], 1.0))
            done(nc.gpsimd.memset(averager[:], 1.0 / 128))
            done(nc.gpsimd.memset(power[:], -0.5))
            nc.gpsimd.memset(half_eps[:], EPS).then_inc(s_setup, 1)
            def add_bias(n, j, low):
                pool.wait_ge(p_xt, n + 1)
                pool.wait_ge(v_pool, n + 1)
                pool.wait_ge(g_xl, low)
                nc.gpsimd.tensor_tensor(x_in[j][:], x_in[j][:], out_bias[:, None, :].to_broadcast([128, 4, C]),
                                        ALU.add).then_inc(g_bias, 1)

            def scale_probs(n, low):
                pool.wait_ge(v_inv, n + 1)
                pool.wait_ge(g_xl, low)
                flat = scores[:].rearrange("p g h n -> p (g h) n")
                nc.gpsimd.tensor_tensor(flat, flat, inverse[:, :, None].to_broadcast([128, PAIRS * HEADS, NK]),
                                        ALU.mult).then_inc(g_probs, 1)

            def spread_keys(n):
                pool.wait_ge(v_ks, n + 1)
                pool.wait_ge(p_s, n)
                pool.wait_ge(g_xl, 2 * n + 2)
                pool.wait_ge(g_probs, n)
                for k, (t, source, mask, heads) in enumerate(((kbd_a, ks_a, mask_a, HA), (kbd_b, ks_b, mask_b, HB))):
                    wide = [128, 2 * WB, heads, NK]
                    pool.wait_ge(g_kbd, 2 * n + k)
                    nc.gpsimd.tensor_tensor(
                        t[:].rearrange("p s w h n -> p (s w) h n"),
                        source[:].rearrange("p s (w n) -> p (s w) n", n=NK)[:, :, None, :].to_broadcast(wide),
                        mask[:, None, :, :].to_broadcast(wide), ALU.mult).then_inc(g_kbd, 1)

            def low_keys(n):
                pool.wait_ge(v_dh, n + 1)
                pool.wait_ge(g_kbd, 2 * n)
                nc.gpsimd.tensor_tensor(dl_a[:], zd_a[:], dh_a[:], ALU.subtract).then_inc(g_dl, 1)
                pool.wait_ge(g_dl, 2 * n + 1)
                nc.gpsimd.tensor_tensor(ds_b[CB:128, :], zd_b[:], ds_b[0:CB, :], ALU.subtract).then_inc(g_dl, 1)

            def low_x(n, k):
                pool.wait_ge(v_xh, n + 1)
                pool.wait_ge(g_dl, 2 * n + 2)
                nc.gpsimd.tensor_tensor(xl_a[:, k], z_a[:], xh_a[:, k], ALU.subtract).then_inc(g_xl, 1)
                pool.wait_ge(g_xl, 2 * n + 1)
                nc.gpsimd.tensor_tensor(xs_b[CB:128, k], z_b[:], xs_b[0:CB, k], ALU.subtract).then_inc(g_xl, 1)

            pool.wait_ge(s_out_bias, 16)
            with pool.Fori(0, B) as b:
                pool.wait_ge(v_var, b + 1)
                nc.gpsimd.tensor_tensor(group_mv[:, 1, :], spread[:], power[:], ALU.pow).then_inc(g_rstd, 1)
                first = b * (ROWS * BLOCKS)
                low_keys(first)
                low_x(first, 0)
                spread_keys(first)
                add_bias(first, 0, 2 * first + 2)
                scale_probs(first, 2 * first + 2)
                low_keys(first + 1)
                low_x(first + 1, 1)
                spread_keys(first + 1)

                def step(n, j):
                    low_keys(n + 2)
                    low_x(n + 2, j % 2)
                    add_bias(n + 1, (j + 1) % BLOCKS, 2 * n + 6)
                    scale_probs(n + 1, 2 * n + 6)
                    spread_keys(n + 2)

                with pool.Fori(0, ROWS - 1) as i:
                    for j in range(BLOCKS):
                        step((b * ROWS + i) * BLOCKS + j, j)
                for j in range(BLOCKS - 2):
                    step((b * ROWS + ROWS - 1) * BLOCKS + j, j)
                last = b * (ROWS * BLOCKS) + ROWS * BLOCKS - 1
                add_bias(last, BLOCKS - 1, 2 * last + 2)
                scale_probs(last, 2 * last + 2)

        @block.vector
        def _(dve):
            steps = [0]

            def done(ins):
                steps[0] += 1
                ins.then_inc(s_setup_v, 1)
                dve.wait_ge(s_setup_v, steps[0])

            for t in (*w16.values(), v_bias, ks_b):
                done(nc.vector.memset(t[:], 0.0))
            for k, n in enumerate("qkvo"):
                t = w16[n]
                dve.wait_ge(s_weight, 16 * 3 * (k + 1))
                for w in (w32_a, w32_b):
                    done(nc.vector.tensor_scalar(w[:], w[:], UP, None, ALU.mult))
                rest = slice(0, CB) if n != "o" else slice(CB, 128)
                for slot, w, rows in ((0, w32_a, slice(0, 128)), (2, w32_b, slice(0, 128))):
                    done(nc.vector.tensor_copy(t[:, slot, 0:C], w[:]))
                    rows = rows if slot == 0 else rest
                    done(nc.vector.tensor_tensor(t[rows, slot + 1, 0:C], w[rows, :], t[rows, slot, 0:C], ALU.subtract))
                if n == "k":
                    done(nc.vector.tensor_copy(t[:, :, C:C + CB], t[:, :, CA:C]))
                nc.vector.memset(top[:, 0:1], 0.0).then_inc(s_split, 1)
                dve.wait_ge(s_split, k + 1)
            dve.wait_ge(s_vector, 16 * 7)
            done(nc.vector.tensor_scalar(qk_bias[:], qk_bias[:], UP, None, ALU.mult))
            done(nc.vector.tensor_scalar(v_bias32[:], v_bias32[:], UP, None, ALU.mult))
            done(nc.vector.tensor_copy(v_bias[0:1], v_bias32[:]))
            done(nc.vector.tensor_tensor(v_bias[32:33], v_bias32[:], v_bias[0:1], ALU.subtract))

            def take_in(k, row, groups):
                for g in groups:
                    last = nc.vector.bn_stats(stats[:, g, row, :], stat_x[k][:, :, GC * g:GC * g + GC])
                return last

            with dve.Fori(0, ROWS // 2) as i:
                for k in range(2):
                    dve.wait_ge(s_stat[k], 16 * i + 16)
                    take_in(k, 2 * i + k, range(GROUPS)).then_inc(v_stat[k], 1)

            dve.wait_ge(s_setup, 1)
            dve.wait_ge(s_bias, 16 * 64)
            iv = ident[:].rearrange("p (r x a y c) -> p r x a y c", r=8, x=2, a=2, y=2, c=2)
            for k, view in enumerate((iv[:, :, :, :, 1, :].rearrange("p r x a c -> p (r x a) c"),
                                      iv[:, :, 1].rearrange("p r a y c -> p r (a y c)"))):
                done(nc.vector.tensor_reduce(top[:, k:k + 1], view, AX.XY, ALU.add))
            for c in range(2):
                done(nc.vector.tensor_scalar(top[:, 2 + c:3 + c], top[:, c:c + 1], -BIG, None, ALU.mult))
                done(nc.vector.tensor_scalar(top[:, 4 + c:5 + c], top[:, c:c + 1], BIG, -BIG, ALU.mult, ALU.add))
            rm = row_mask[:, 1].rearrange("p h (x y z) -> p (h x) y z", x=4, y=2)
            cm = col_mask[:].rearrange("p h (x z) -> p h x z", x=2)
            done(nc.vector.tensor_scalar(rm[:, :, 0], rm[:, :, 0], top[:, 2:3], None, ALU.add))
            done(nc.vector.tensor_scalar(rm[:, :, 1], rm[:, :, 1], top[:, 4:5], None, ALU.add))
            done(nc.vector.tensor_scalar(cm[:, :, 0], cm[:, :, 0], top[:, 3:4], None, ALU.add))
            done(nc.vector.tensor_scalar(cm[:, :, 1], cm[:, :, 1], top[:, 5:6], None, ALU.add))
            done(nc.vector.tensor_copy(mask_a[:], head_mask[:, 0:HA, None].to_broadcast([128, HA, NK])))
            done(nc.vector.tensor_tensor(mask_b[:], head_mask[:, 0:HB, None].to_broadcast([128, HB, NK]),
                                         head_mask[:, HB:2 * HB, None].to_broadcast([128, HB, NK]), ALU.add))
            done(nc.vector.tensor_scalar(bias32[:], bias32[:], 1.0 / SCALE, None, ALU.mult))
            for h in range(HEADS):
                source = bias32[:, h].rearrange("p (y x) -> p x y", x=4)
                high, low = (t[:, h].rearrange("p (x y) -> p x y", x=4) for t in (bias16, bias16_low))
                done(nc.vector.tensor_copy(high, source))
                done(nc.vector.tensor_tensor(low, source, high, ALU.subtract))
            nc.vector.tensor_copy(bias16[64:128], bias16_low[64:128]).then_inc(s_setup, 1)

            def normalisation(b):
                count = [0]

                def link(ins):
                    count[0] += 1
                    ins.then_inc(v_chain, 1)
                    dve.wait_ge(v_chain, 11 * b + count[0])

                dve.wait_ge(v_stat[1], ROWS // 2)
                dve.wait_ge(v_stat[0], ROWS // 2 + b * ROWS)
                nc.vector.memset(norm_b[:], 0.0)
                for g in range(GROUPS):
                    last = nc.vector.bn_aggr(part[:, g, :], stats[:, g].rearrange("p r s -> p (r s)"))
                last.then_inc(v_part, 1)
                dve.wait_ge(v_part, b + 1)
                dve.wait_ge(p_mean, b + 1)
                link(nc.vector.tensor_scalar(group_mv[:, 0, :], ps[:, BV + 1, 0:GROUPS], -1.0, None, ALU.mult))
                link(nc.vector.tensor_tensor(group_tmp[:], part[:, :, 0], group_mv[:, 0, :], ALU.add))
                link(nc.vector.tensor_tensor(group_tmp[:], group_tmp[:], group_tmp[:], ALU.mult))
                nc.vector.tensor_tensor(group_tmp[:], group_tmp[:], part[:, :, 1], ALU.add).then_inc(v_dev, 1)
                dve.wait_ge(p_var, b + 1)
                nc.vector.tensor_tensor(spread[:], ps[:, BV + 1, GROUPS:2 * GROUPS], half_eps[:], ALU.add).then_inc(v_var, 1)
                dve.wait_ge(g_rstd, b + 1)
                for k, (which, chunk) in enumerate(((1, 0), (1, 1), (0, 0), (0, 1))):
                    link(nc.vector.tensor_tensor(picked[:, k, :], group_mv[:, which, :], pick[:, chunk, :], ALU.mult))
                for k in range(4):
                    link(nc.vector.tensor_reduce(norm[:, k:k + 1], picked[:, k, :], AX.X, ALU.add))
                nc.vector.tensor_tensor(norm_b[:], norm[:, 0:2], norm[:, 2:4], ALU.mult).then_inc(v_norm, 1)


            def pool_keys(n, j, arrived):
                dve.wait_ge(s_x[j], arrived)
                dve.wait_ge(v_pool, n)
                nc.vector.tensor_tensor(pool_dx[:], x_in[j][:, 0:4:2, :], x_in[j][:, 1:4:2, :], ALU.max).then_inc(v_pool1, 1)
                dve.wait_ge(v_pool1, n + 1)
                dve.wait_ge(p_kx, n)
                nc.vector.tensor_tensor(pooled[:], pool_dx[:, 0], pool_dx[:, 1], ALU.max).then_inc(v_pool, 1)

            def high_keys(n):
                dve.wait_ge(a_zd, n + 1)
                dve.wait_ge(p_kv, n)
                nc.vector.tensor_copy(dh_a[:], zd_a[:])
                nc.vector.tensor_copy(ds_b[0:CB, :], zd_b[:]).then_inc(v_dh, 1)

            def high_x(n, k, used):
                dve.wait_ge(a_z, n + 1)
                dve.wait_ge(p_q, used)
                nc.vector.tensor_copy(xh_a[:, k], z_a[:])
                nc.vector.tensor_copy(xs_b[0:CB, k], z_b[:]).then_inc(v_xh, 1)

            def keys_values(n):
                dve.wait_ge(a_kv, n + 1)
                dve.wait_ge(g_kbd, 2 * n)
                nc.vector.scalar_tensor_tensor(ks_a[:, 1, :], ps[:, BK, 0:KEYS], qk_bias[:, 2:3], ks_a[:, 0, :],
                                               ALU.add, ALU.subtract)
                nc.vector.scalar_tensor_tensor(ks_b[0:CB, 1, :], ps[0:CB, BK, KEYS:2 * KEYS], qk_bias[0:CB, 3:4],
                                               ks_b[0:CB, 0, :], ALU.add, ALU.subtract).then_inc(v_ks, 1)
                nc.vector.tensor_tensor(v16[:, 1, :], ps[:, BK, 2 * KEYS:2 * KEYS + C], v16[:, 0, :],
                                        ALU.subtract).then_inc(v_v, 1)

            def queries(n):
                dve.wait_ge(a_qa, n + 1)
                nc.vector.scalar_tensor_tensor(ql_a[:], ps[:, BQ, :], qk_bias[:, 0:1], qh_a[:], ALU.add, ALU.subtract)
                for half in range(2):
                    cols = slice(TOK // 2 * half, TOK // 2 * (half + 1))
                    dve.wait_ge(a_qb, 2 * n + half + 1)
                    last = nc.vector.scalar_tensor_tensor(
                        qs_b[CB:128, cols], ps[CB * half:CB * half + CB, BQ + 1, 0:TOK // 2],
                        qk_bias[CB * half:CB * half + CB, 1:2], qs_b[0:CB, cols], ALU.add, ALU.subtract)
                last.then_inc(v_q, 1)

            def probs_low(n):
                dve.wait_ge(a_pt, n + 1)
                dve.wait_ge(p_av, n)
                nc.vector.tensor_tensor(pl[:], ps[0:HK, BS, :], ph[:], ALU.subtract).then_inc(v_pt, 1)

            def attended_low(n):
                dve.wait_ge(p_wo, 2 * n)
                dve.wait_ge(a_ava, n + 1)
                nc.vector.tensor_tensor(al_a[:], ps[:, BX, :], ah_a[:], ALU.subtract)
                dve.wait_ge(a_avb, n + 1)
                nc.vector.tensor_tensor(as_b[0:CB, :], ps[CB:128, BX + 1, :], as_b[CB:128, :],
                                        ALU.subtract).then_inc(v_av, 1)

            flat = scores[:].rearrange("p g h n -> p (g h) n")
            wide = [128, PAIRS * HEADS, NK]

            def softmax_head(n):
                source = ps[:, BS, 0:PAIRS * HK].rearrange("p (a n) -> p a n", n=NK)
                dve.wait_ge(p_s, n + 1)
                dve.wait_ge(v_sub, n)
                nc.vector.tensor_reduce(top[:], source, AX.X, ALU.max).then_inc(v_max, 1)
                dve.wait_ge(v_max, n + 1)
                dve.wait_ge(p_pt, n)
                nc.vector.tensor_tensor(flat, source, top[:, :, None].to_broadcast(wide), ALU.subtract).then_inc(v_sub, 1)

            def softmax_tail(n):
                dve.wait_ge(a_exp, n + 1)
                dve.wait_ge(v_inv, n)
                nc.vector.tensor_reduce(total[:], flat, AX.X, ALU.add).then_inc(v_sum, 1)
                dve.wait_ge(v_sum, n + 1)
                dve.wait_ge(g_probs, n)
                nc.vector.reciprocal(inverse[:], total[:]).then_inc(v_inv, 1)

            def add_input(n, j, k, stored):
                dve.wait_ge(p_wo, 2 * n + k + 1)
                if k == 0:
                    dve.wait_ge(g_bias, n + 1)
                    dve.wait_ge(s_o[j], stored)
                nc.vector.scalar_tensor_tensor(x_out[j][:, 2 * k:2 * k + 2, :],
                                               ps[:, BQ + k, 0:2 * C].rearrange("p (m c) -> p m c", m=2),
                                               1.0 / (UP * UP), x_in[j][:, 2 * k:2 * k + 2, :],
                                               ALU.mult, ALU.add).then_inc(v_added[j], 1)

            def statistics(b, i, j, early):
                share = GROUPS // (BLOCKS - 1) + 1
                mine = range(share * j, min(share * (j + 1), GROUPS))
                if early:
                    if j == 0:
                        dve.wait_ge(s_stat[0], 16 * (ROWS // 2 + b * ROWS + i + 1))
                    take_in(0, i, mine[:share // 2])
                else:
                    last = take_in(0, i, mine[share // 2:])
                    if j == BLOCKS - 2:
                        last.then_inc(v_stat[0], 1)

            def row(b, i, with_stats, last_row):
                for j in range(BLOCKS):
                    n = (b * ROWS + i) * BLOCKS + j
                    more = not (last_row and j == BLOCKS - 1)
                    more2 = not (last_row and j >= BLOCKS - 2)
                    if more2:
                        high_x(n + 2, j % 2, n + 1)
                    probs_low(n)
                    if with_stats and j < BLOCKS - 1:
                        statistics(b, i, j, True)
                    if more2:
                        high_keys(n + 2)
                    if more:
                        queries(n + 1)
                    if with_stats and j < BLOCKS - 1:
                        statistics(b, i, j, False)
                    attended_low(n)
                    if more:
                        softmax_head(n + 1)
                    if j == 0:
                        pool_keys(n + 3, j + 3, counted(j + 3, b, i + 1, int(last_row)))
                    elif not last_row:
                        pool_keys(n + 3, j - 1, counted(j - 1, b, i + 2, (i + 2) // ROWS))
                    if more:
                        softmax_tail(n + 1)
                    if more2:
                        keys_values(n + 2)
                    add_input(n, j, 0, counted(j, b, i))
                    add_input(n, j, 1, counted(j, b, i))

            def image(b, with_stats):
                normalisation(b)
                n = b * ROWS * BLOCKS
                for j in range(2):
                    pool_keys(n + j, j, counted(j, b, 1))
                    high_keys(n + j)
                    high_x(n + j, j, n)
                    keys_values(n + j)
                    if j == 0:
                        queries(n)
                        softmax_head(n)
                        softmax_tail(n)
                pool_keys(n + 2, 2, counted(2, b, 1))
                with dve.Fori(0, ROWS - 1) as i:
                    row(b, i, with_stats, False)
                row(b, ROWS - 1, with_stats, True)

            with dve.Fori(0, B - 1) as b:
                image(b, True)
            image(B - 1, False)

        @block.scalar
        def _(act):
            def norm_x(n):
                act.wait_ge(p_xt, n + 1)
                act.wait_ge(v_xh, n)
                act.wait_ge(g_xl, 2 * n)
                nc.scalar.activation(z_a[:], ps[:, BX, :], ACT.Identity, bias=norm_b[:, 0:1], scale=norm[:, 0:1])
                nc.scalar.activation(z_b[:], ps[0:CB, BX + 1, :], ACT.Identity,
                                     bias=norm_b[0:CB, 1:2], scale=norm[0:CB, 1:2]).then_inc(a_z, 1)

            def norm_keys(n):
                act.wait_ge(p_kx, n + 1)
                act.wait_ge(v_dh, n)
                act.wait_ge(g_dl, 2 * n)
                nc.scalar.activation(zd_a[:], ps[:, BK, 0:KEYS], ACT.Identity, bias=norm_b[:, 0:1], scale=norm[:, 0:1])
                nc.scalar.activation(zd_b[:], ps[0:CB, BK, KEYS:2 * KEYS], ACT.Identity,
                                     bias=norm_b[0:CB, 1:2], scale=norm[0:CB, 1:2]).then_inc(a_zd, 1)

            def keys_values(n):
                act.wait_ge(p_kv, n + 1)
                act.wait_ge(g_kbd, 2 * n)
                act.wait_ge(p_sel, WB * n)
                nc.scalar.activation(ks_a[:, 0, :], ps[:, BK, 0:KEYS], ACT.Identity, bias=qk_bias[:, 2:3])
                nc.scalar.activation(ks_b[:, 0, :], ps[:, BK, KEYS:2 * KEYS], ACT.Identity, bias=qk_bias[:, 3:4])
                nc.scalar.activation(v16[:, 0, :], ps[:, BK, 2 * KEYS:2 * KEYS + C], ACT.Copy).then_inc(a_kv, 1)

            def queries_a(n):
                act.wait_ge(p_qa, n + 1)
                act.wait_ge(p_s, n)
                nc.scalar.activation(qh_a[:], ps[:, BQ, :], ACT.Identity, bias=qk_bias[:, 0:1]).then_inc(a_qa, 1)

            def queries_b(n):
                act.wait_ge(p_q, n + 1)
                for half in range(2):
                    nc.scalar.activation(qs_b[0:CB, TOK // 2 * half:TOK // 2 * (half + 1)],
                                         ps[CB * half:CB * half + CB, BQ + 1, 0:TOK // 2],
                                         ACT.Identity, bias=qk_bias[CB * half:CB * half + CB, 1:2]).then_inc(a_qb, 1)

            def values(n, k, windows, used):
                act.wait_ge(p_av, used)
                for w in windows:
                    act.wait_ge(p_sel, WB * n + w + 1)
                    nc.scalar.activation(vbd[:, k, w].rearrange("p s c -> p (s c)"),
                                         ps[0:HK, BV + w % 2, 0:2 * C], ACT.Copy).then_inc(a_sel, 1)

            def exps(n):
                act.wait_ge(v_sub, n + 1)
                nc.scalar.activation(scores[:].rearrange("p g h n -> p (g h n)"),
                                     scores[:].rearrange("p g h n -> p (g h n)"), ACT.Exp,
                                     scale=SCALE / (UP * UP)).then_inc(a_exp, 1)

            def probs(n):
                act.wait_ge(p_pt, n + 1)
                act.wait_ge(p_av, n)
                nc.scalar.activation(ph[:], ps[0:HK, BS, :], ACT.Copy).then_inc(a_pt, 1)

            def attended(n):
                act.wait_ge(p_av, n + 1)
                act.wait_ge(p_wo, 2 * n)
                nc.scalar.activation(ah_a[:], ps[:, BX, :], ACT.Copy).then_inc(a_ava, 1)
                nc.scalar.activation(as_b[CB:128, :], ps[CB:128, BX + 1, :], ACT.Copy).then_inc(a_avb, 1)

            def row(b, i, last_row):
                for j in range(BLOCKS):
                    n = (b * ROWS + i) * BLOCKS + j
                    more = not (last_row and j == BLOCKS - 1)
                    more2 = not (last_row and j >= BLOCKS - 2)
                    if more2:
                        norm_x(n + 2)
                    probs(n)
                    if more:
                        values(n + 1, (j + 1) % 2, range(0, 2), n)
                    if more2:
                        norm_keys(n + 2)
                    if more:
                        queries_a(n + 1)
                        queries_b(n + 1)
                        values(n + 1, (j + 1) % 2, range(2, 4), n)
                    attended(n)
                    if more:
                        values(n + 1, (j + 1) % 2, range(4, 6), n)
                        exps(n + 1)
                        values(n + 1, (j + 1) % 2, range(6, 8), n)
                    if more2:
                        keys_values(n + 2)

            def image(b):
                n = b * ROWS * BLOCKS
                act.wait_ge(v_norm, b + 1)
                norm_keys(n)
                norm_x(n)
                keys_values(n)
                values(n, 0, range(WB), n)
                queries_a(n)
                queries_b(n)
                exps(n)
                norm_keys(n + 1)
                norm_x(n + 1)
                keys_values(n + 1)
                with act.Fori(0, ROWS - 1) as i:
                    row(b, i, False)
                row(b, ROWS - 1, True)

            with act.Fori(0, B) as b:
                image(b)

        @block.tensor
        def _(pe):
            def mm(o, left, right, start, stop):
                return nc.tensor.matmul(o, left, right, start=start, stop=stop, skip_group_check=True)

            def tokens(t, w):
                return t.rearrange("p (m w c) -> p m w c", w=WB, c=NK)[:, :, w, :]

            def transposes(n, j, arrived):
                pe.wait_ge(s_x[j], arrived)
                for m in range(4):
                    columns = [ps[0:rows, BX + k, :].rearrange("p (w m c) -> p w m c", w=WB, c=NK)[:, :, m, :]
                               for k, rows in enumerate((CA, CB))]
                    nc.tensor.transpose(columns[0], x_in[j][:, m, 0:CA], ident[:])
                    last = nc.tensor.transpose(columns[1], x_in[j][:, m, CA:C], ident[:])
                last.then_inc(p_xt, 1)

            def transpose_keys(n):
                pe.wait_ge(v_pool, n + 1)
                pe.wait_ge(v_v, n)
                nc.tensor.transpose(ps[0:CA, BK, 0:KEYS], pooled[:, 0:CA], ident[:])
                nc.tensor.transpose(ps[0:CB, BK, KEYS:2 * KEYS], pooled[:, CA:C], ident[:]).then_inc(p_kx, 1)

            def products(o, pairs):
                for k, (left, right) in enumerate(pairs):
                    last = mm(o, left, right, k == 0, k == len(pairs) - 1)
                return last

            def project_keys(n):
                pe.wait_ge(v_dh, n + 1)
                pe.wait_ge(g_dl, 2 * n + 2)
                operand = [(0, dh_a), (1, dh_a), (0, dl_a), (2, ds_b), (3, ds_b)]
                for lo in (0, CA):
                    products(ps[:, BK, lo:lo + KEYS], [(w16["k"][:, s, lo:lo + 128], t[:]) for s, t in operand])
                products(ps[:, BK, 2 * KEYS:2 * KEYS + C], [(ones_rows[:], v_bias[:])] +
                         [(t[:], w16["v"][:, s, :]) for s, t in operand]).then_inc(p_kv, 1)

            def query_operand(k):
                return [(0, xh_a[:, k]), (1, xh_a[:, k]), (2, xs_b[:, k]), (3, xs_b[:, k]), (0, xl_a[:, k])]

            def project_queries_a(n, k):
                pe.wait_ge(v_xh, n + 1)
                pe.wait_ge(g_xl, 2 * n + 2)
                products(ps[:, BQ, :], [(w16["q"][:, s, 0:CA], t) for s, t in query_operand(k)]).then_inc(p_qa, 1)

            def project_queries_b(k):
                operand = query_operand(k)
                for step, (s, t) in enumerate(operand):
                    for half in range(2):
                        last = mm(ps[CB * half:CB * half + CB, BQ + 1, 0:TOK // 2], w16["q"][:, s, CA:C],
                                  t[:, TOK // 2 * half:TOK // 2 * (half + 1)], step == 0, step == len(operand) - 1)
                last.then_inc(p_q, 1)

            def score(n, rho, j):
                pe.wait_ge(v_sub, n)
                pe.wait_ge(v_pt, n)
                pe.wait_ge(v_q, n + 1)
                pe.wait_ge(g_kbd, 2 * n + 2)
                o = ps[:, BS, 0:PAIRS * HK].rearrange("p (g k) -> p g k", g=PAIRS)
                mm(o, two_ident[:], bias16[:].rearrange("p h n -> p (h n)")[:, None, :].to_broadcast([128, PAIRS, HK]),
                   True, False)
                if rho is not None:
                    flat = row_mask[:].rearrange("p v h n -> p (v h n)")
                    for g in range(PAIRS):
                        mm(o[:, g, :], mask_left[:], flat[:, bass.ds(rho * HK, HK)], False, False)
                if j == BLOCKS - 1:
                    mm(o[:, PAIRS - 1, :], mask_left_last[:], col_mask[:].rearrange("p h n -> p (h n)"), False, False)
                for w in range(WB):
                    p = 64 * (w % 2)
                    cols = slice(NQ * w, NQ * w + NQ)
                    k_high, k_low = (kbd_a[:, s, w].rearrange("p h n -> p (h n)") for s in range(2))
                    for left, right in ((qh_a, k_high), (qh_a, k_low), (ql_a, k_high)):
                        mm(o[p:p + 64, w // 2, 0:HA * NK], left[:, cols], right, False, False)
                    for s in range(2):
                        last = mm(o[p:p + 64, w // 2, HA * NK:HK], qs_b[:, cols],
                                  kbd_b[:, s, w].rearrange("p h n -> p (h n)"), False, s == 1 and w >= WB - 2)
                last.then_inc(p_s, 1)

            def values(n, windows):
                pe.wait_ge(v_v, n + 1)
                for w in windows:
                    pe.wait_ge(a_sel, WB * n + max(w - 1, 0))
                    o = ps[:, BV + w % 2, 0:2 * C].rearrange("p (s c) -> p s c", s=2)
                    for h in range(HEADS):
                        at = 80 - NK * h
                        last = mm(o[:, :, HD * h:HD * h + HD], spread_w[:, w, at:at + 128],
                                  v16[:, :, HD * h:HD * h + HD], True, True)
                    last.then_inc(p_sel, 1)

            def probs(n):
                pe.wait_ge(g_probs, n + 1)
                for g in range(PAIRS):
                    last = nc.tensor.transpose(ps[0:HK, BS, 128 * g:128 * g + 128],
                                               scores[:, g].rearrange("p h n -> p (h n)"), ident[:])
                last.then_inc(p_pt, 1)

            def attend(n, k):
                pe.wait_ge(v_pt, n + 1)
                pe.wait_ge(a_sel, WB * (n + 1))
                pe.wait_ge(v_av, n)
                for w in range(WB):
                    cols = slice(NQ * w, NQ * w + NQ)
                    for bank, c in ((BX, 0), (BX + 1, C - 128)):
                        last = products(tokens(ps[:, bank, :], w), [(vbd[:, k, w, s, c:c + 128], t[:, cols])
                                                            for s, t in ((0, ph), (0, pl), (1, ph))])
                last.then_inc(p_av, 1)

            def project_out(n):
                pe.wait_ge(v_av, n + 1)
                for m in range(4):
                    cols = slice(128 * m, 128 * m + 128)
                    last = products(ps[:, BQ + m // 2, C * (m % 2):C * (m % 2) + C],
                                    [(t[:, cols], w16["o"][:, s, :])
                                     for s, t in ((0, ah_a), (1, ah_a), (0, al_a), (2, as_b), (3, as_b))])
                    if m % 2:
                        last.then_inc(p_wo, 1)

            def row(b, i, last_row):
                for j in range(BLOCKS):
                    n = (b * ROWS + i) * BLOCKS + j
                    more = not (last_row and j == BLOCKS - 1)
                    more2 = not (last_row and j >= BLOCKS - 2)
                    nj = (j + 1) % BLOCKS
                    k = j % 2
                    probs(n)
                    if more2:
                        transpose_keys(n + 2)
                    if more:
                        values(n + 1, range(0, 2))
                        if j:
                            pe.wait_ge(v_added[j - 1], 2 * (b * ROWS + i) + 1)
                        else:
                            pe.wait_ge(v_added[BLOCKS - 1], 2 * (b * ROWS + i))
                        project_queries_a(n + 1, 1 - k)
                        if j:
                            pe.wait_ge(v_added[j - 1], 2 * (b * ROWS + i + 1))
                        project_queries_b(1 - k)
                        values(n + 1, range(2, 4))
                    if more2:
                        pe.wait_ge(a_z, n + 3)
                    attend(n, k)
                    if more:
                        values(n + 1, range(4, 6))
                        if last_row:
                            score(n + 1, 1, nj)
                        elif nj:
                            score(n + 1, None, nj)
                        else:
                            score(n + 1, (i + 2) // ROWS, nj)
                        values(n + 1, range(6, 8))
                    if more2:
                        project_keys(n + 2)
                    pe.wait_ge(v_av, n + 1)
                    if j == 0:
                        transposes(n + 3, j + 3, counted(j + 3, b, i + 1, int(last_row)))
                    elif not last_row:
                        transposes(n + 3, j - 1, counted(j - 1, b, i + 2, (i + 2) // ROWS))
                    project_out(n)

            def image(b):
                n = b * ROWS * BLOCKS
                pe.wait_ge(v_part, b + 1)
                pe.wait_ge(a_sel, WB * n)
                mm(ps[:, BV + 1, 0:GROUPS], averager[:], part[:, :, 0], True, True).then_inc(p_mean, 1)
                pe.wait_ge(v_dev, b + 1)
                mm(ps[:, BV + 1, GROUPS:2 * GROUPS], averager[:], group_tmp[:], True, True).then_inc(p_var, 1)
                pe.wait_ge(v_av, n)
                pe.wait_ge(v_added[BLOCKS - 1], 2 * b * ROWS)
                transposes(n, 0, counted(0, b, 1))
                transpose_keys(n)
                project_keys(n)
                values(n, range(WB))
                project_queries_a(n, 0)
                project_queries_b(0)
                score(n, None, 0)
                pe.wait_ge(a_z, n + 1)
                transposes(n + 1, 1, counted(1, b, 1))
                transpose_keys(n + 1)
                project_keys(n + 1)
                pe.wait_ge(a_z, n + 2)
                transposes(n + 2, 2, counted(2, b, 1))
                with pe.Fori(0, ROWS - 1) as i:
                    row(b, i, False)
                row(b, ROWS - 1, True)

            pe.wait_ge(s_setup, 2)
            with pe.Fori(0, B) as b:
                image(b)


_INS = ["x", "Wq", "bq", "Wk", "bk", "Wv", "bv", "Wo", "bo"]


def kernel(**inputs):
    import concourse.bacc as bacc
    from concourse.bass_utils import run_bass_kernel_spmd

    nc = bacc.Bacc("TRN2", target_bir_lowering=False, num_devices=1)
    arrays = {"x": np.ascontiguousarray(inputs["x"])}
    for name in _INS[1:]:
        arrays[name] = np.ascontiguousarray(inputs["L0_conv_" + name])
    arrays["table"] = np.ascontiguousarray(inputs["L0_conv_rel_table"][:, :, ::-1])
    args = [nc.dram_tensor(n, a.shape, mybir.dt.from_np(a.dtype), kind="ExternalInput").ap() for n, a in arrays.items()]
    args.append(nc.dram_tensor("y", arrays["x"].shape, F32, kind="ExternalOutput").ap())
    attention_kernel(nc, *args)
    result = run_bass_kernel_spmd(nc, [arrays], core_ids=[0])
    return result.results[0]["y"]
```
